# Optimizing a Trainium2 kernel written in Bass

```python
import numpy as np
import jax
import jax.numpy as jnp

def _softmax(x, axis=-1):
    return jax.nn.softmax(x, axis=axis)

def _gelu(x):
    return jax.nn.gelu(x, approximate=True)

def _silu(x):
    return jax.nn.silu(x)

def _sigmoid(x):
    return jax.nn.sigmoid(x)

def _layernorm(x, axis=-1, eps=1e-05):
    m = jnp.mean(x, axis=axis, keepdims=True)
    v = jnp.var(x, axis=axis, keepdims=True)
    return (x - m) / jnp.sqrt(v + eps)

def _scatter_add(tgt, idx, src, axis=0):
    return tgt.at[idx].add(src)

def _segment_sum(src, seg, n):
    return jax.ops.segment_sum(src, seg, n)
kernel_name = 'mk_conv_preact_d2_conv_nchw256_r4_79ef8e'

def setup_inputs(seed: int=0):
    np.random.seed(seed)
    _w = jnp.asarray

    def _rec_inputs():
        import jax
        import jax.numpy as jnp
        _gk = jax.random.key(seed)
        x = 7.22e-05 + 1 * jax.random.normal(jax.random.fold_in(_gk, 1), (8, 64, 16, 16), jnp.float32)
        return x
    x = _rec_inputs()

    def _L0_conv_setup():
        import jax, jax.numpy as jnp
        import numpy as np
        N_, C_, H_, W_ = (8, 64, 16, 16)
        HEADS = 8
        KS = 3
        K2 = KS * KS
        OUT = 64
        HD = OUT // HEADS
        STRIDE = 1
        PAD = 1

        def _conv2d(x, w, b):
            out = jax.lax.conv_general_dilated(x, w, (STRIDE, STRIDE), [(PAD, PAD), (PAD, PAD)], dimension_numbers=('NCHW', 'OIHW', 'NCHW'))
            return out + b[None, :, None, None]
        key = jax.random.key(seed)
        ks = jax.random.split(key, 8)
        s = 0.05
        return {'input_features': jax.random.normal(ks[0], (N_, C_, H_, W_), jnp.float32), 'Wq': jax.random.normal(ks[1], (OUT, C_), jnp.float32) * s, 'Wk': jax.random.normal(ks[2], (OUT, C_), jnp.float32) * s, 'Wv': jax.random.normal(ks[3], (OUT, C_), jnp.float32) * s, 'off_w': jax.random.normal(ks[4], (HEADS * K2 * 2, C_, KS, KS), jnp.float32) * 0.01, 'off_b': jnp.zeros((HEADS * K2 * 2,), jnp.float32), 'attn_w': jax.random.normal(ks[5], (HEADS * K2, C_, KS, KS), jnp.float32) * 0.01, 'attn_b': jnp.zeros((HEADS * K2,), jnp.float32), 'Wo': jax.random.normal(ks[6], (OUT, OUT), jnp.float32) * s}
    _L0_conv_all = _L0_conv_setup()
    _L0_conv_in = {k: v for k, v in _L0_conv_all.items() if k in ('Wq', 'Wk', 'Wv', 'off_w', 'off_b', 'attn_w', 'attn_b', 'Wo')}
    del _L0_conv_all

    def _L1_conv_setup():
        import jax, jax.numpy as jnp
        import numpy as np
        from jax import lax
        EPS = 1e-05
        GROUPS = 32

        def conv2d(x, w, padding):
            return lax.conv_general_dilated(x, w, window_strides=(1, 1), padding=[(padding, padding), (padding, padding)], dimension_numbers=('NCHW', 'OIHW', 'NCHW'))

        def group_norm(x, gamma, beta):
            B, C, H, W = x.shape
            xg = x.reshape(B, GROUPS, C // GROUPS, H, W)
            mean = xg.mean(axis=(2, 3, 4), keepdims=True)
            var = xg.var(axis=(2, 3, 4), keepdims=True)
            xn = ((xg - mean) * lax.rsqrt(var + EPS)).reshape(B, C, H, W)
            return xn * gamma[None, :, None, None] + beta[None, :, None, None]

        def top_pool(x):
            return lax.cummax(x, axis=2, reverse=True)

        def left_pool(x):
            return lax.cummax(x, axis=3, reverse=True)
        key = jax.random.key(seed)
        ks = jax.random.split(key, 8)
        B, dim, H, W = (8, 64, 32, 32)
        cdim = 32
        s = lambda fan: 1.0 / np.sqrt(fan)
        return {'x': jax.random.normal(ks[0], (B, dim, H, W), jnp.float32), 'p1_w': jax.random.normal(ks[1], (cdim, dim, 3, 3), jnp.float32) * s(dim * 9), 'p1_b': jnp.zeros((cdim,), jnp.float32), 'p2_w': jax.random.normal(ks[2], (cdim, dim, 3, 3), jnp.float32) * s(dim * 9), 'p2_b': jnp.zeros((cdim,), jnp.float32), 'p_w': jax.random.normal(ks[3], (dim, cdim, 3, 3), jnp.float32) * s(cdim * 9), 'p_gn_g': jnp.ones((dim,), jnp.float32), 'p_gn_b': jnp.zeros((dim,), jnp.float32), 'c1_w': jax.random.normal(ks[4], (dim, dim, 1, 1), jnp.float32) * s(dim), 'gn1_g': jnp.ones((dim,), jnp.float32), 'gn1_b': jnp.zeros((dim,), jnp.float32), 'c2_w': jax.random.normal(ks[5], (dim, dim, 3, 3), jnp.float32) * s(dim * 9), 'c2_b': jnp.zeros((dim,), jnp.float32)}
    _L1_conv_all = _L1_conv_setup()
    _L1_conv_in = {k: v for k, v in _L1_conv_all.items() if k in ('p1_w', 'p1_b', 'p2_w', 'p2_b', 'p_w', 'p_gn_g', 'p_gn_b', 'c1_w', 'gn1_g', 'gn1_b', 'c2_w', 'c2_b')}
    del _L1_conv_all
    return {'x': x, 'L0_conv_Wq': _L0_conv_in['Wq'], 'L0_conv_Wk': _L0_conv_in['Wk'], 'L0_conv_Wv': _L0_conv_in['Wv'], 'L0_conv_off_w': _L0_conv_in['off_w'], 'L0_conv_off_b': _L0_conv_in['off_b'], 'L0_conv_attn_w': _L0_conv_in['attn_w'], 'L0_conv_attn_b': _L0_conv_in['attn_b'], 'L0_conv_Wo': _L0_conv_in['Wo'], 'L1_conv_p1_w': _L1_conv_in['p1_w'], 'L1_conv_p1_b': _L1_conv_in['p1_b'], 'L1_conv_p2_w': _L1_conv_in['p2_w'], 'L1_conv_p2_b': _L1_conv_in['p2_b'], 'L1_conv_p_w': _L1_conv_in['p_w'], 'L1_conv_p_gn_g': _L1_conv_in['p_gn_g'], 'L1_conv_p_gn_b': _L1_conv_in['p_gn_b'], 'L1_conv_c1_w': _L1_conv_in['c1_w'], 'L1_conv_gn1_g': _L1_conv_in['gn1_g'], 'L1_conv_gn1_b': _L1_conv_in['gn1_b'], 'L1_conv_c2_w': _L1_conv_in['c2_w'], 'L1_conv_c2_b': _L1_conv_in['c2_b']}

def reference(x, L0_conv_Wq, L0_conv_Wk, L0_conv_Wv, L0_conv_off_w, L0_conv_off_b, L0_conv_attn_w, L0_conv_attn_b, L0_conv_Wo, L1_conv_p1_w, L1_conv_p1_b, L1_conv_p2_w, L1_conv_p2_b, L1_conv_p_w, L1_conv_p_gn_g, L1_conv_p_gn_b, L1_conv_c1_w, L1_conv_gn1_g, L1_conv_gn1_b, L1_conv_c2_w, L1_conv_c2_b):
    import jax
    import jax.numpy as jnp

    def _L0_conv_ref(input_features, Wq, Wk, Wv, off_w, off_b, attn_w, attn_b, Wo):
        import jax, jax.numpy as jnp
        import numpy as np
        N_, C_, H_, W_ = (8, 64, 16, 16)
        HEADS = 8
        KS = 3
        K2 = KS * KS
        OUT = 64
        HD = OUT // HEADS
        STRIDE = 1
        PAD = 1

        def _conv2d(x, w, b):
            out = jax.lax.conv_general_dilated(x, w, (STRIDE, STRIDE), [(PAD, PAD), (PAD, PAD)], dimension_numbers=('NCHW', 'OIHW', 'NCHW'))
            return out + b[None, :, None, None]
        x = input_features
        N, C, H, W = x.shape
        q = jnp.einsum('oc,nchw->nohw', Wq, x)
        k = jnp.einsum('oc,nchw->nohw', Wk, x)
        v = jnp.einsum('oc,nchw->nohw', Wv, x)
        offsets = _conv2d(x, off_w, off_b)
        aw = jax.nn.sigmoid(_conv2d(x, attn_w, attn_b))
        Ho, Wo_sp = (offsets.shape[2], offsets.shape[3])
        gx_base = jnp.linspace(-1.0, 1.0, Wo_sp)
        gy_base = jnp.linspace(-1.0, 1.0, Ho)
        off = offsets.reshape(N, HEADS, K2, 2, Ho, Wo_sp)
        gx = gx_base[None, None, None, None, :] + off[:, :, :, 0] * (2.0 / W)
        gy = gy_base[None, None, None, :, None] + off[:, :, :, 1] * (2.0 / H)
        xp = (gx + 1.0) * 0.5 * (W - 1)
        yp = (gy + 1.0) * 0.5 * (H - 1)
        x0 = jnp.floor(xp).astype(jnp.int32)
        y0 = jnp.floor(yp).astype(jnp.int32)
        x1 = x0 + 1
        y1 = y0 + 1
        wx1 = xp - x0
        wx0 = 1.0 - wx1
        wy1 = yp - y0
        wy0 = 1.0 - wy1
        vf = v.reshape(N, HEADS, HD, H * W)

        def corner(yi, xi, wgt):
            valid = ((yi >= 0) & (yi < H) & (xi >= 0) & (xi < W)).astype(v.dtype)
            idx = (jnp.clip(yi, 0, H - 1) * W + jnp.clip(xi, 0, W - 1)).reshape(N, HEADS, -1)
            g = jnp.take_along_axis(vf, idx[:, :, None, :], axis=3)
            g = g.reshape(N, HEADS, HD, K2, Ho, Wo_sp)
            return g * (wgt * valid)[:, :, None]
        sampled = corner(y0, x0, wy0 * wx0) + corner(y0, x1, wy0 * wx1) + corner(y1, x0, wy1 * wx0) + corner(y1, x1, wy1 * wx1)
        awr = aw.reshape(N, HEADS, K2, Ho, Wo_sp)
        head_out = jnp.einsum('nhckxy,nhkxy->nhcxy', sampled, awr)
        combined = head_out.reshape(N, OUT, Ho, Wo_sp)
        return jnp.einsum('oc,nchw->nohw', Wo, combined)

    def _L1_conv_ref(x, p1_w, p1_b, p2_w, p2_b, p_w, p_gn_g, p_gn_b, c1_w, gn1_g, gn1_b, c2_w, c2_b):
        import jax, jax.numpy as jnp
        import numpy as np
        from jax import lax
        EPS = 1e-05
        GROUPS = 32

        def conv2d(x, w, padding):
            return lax.conv_general_dilated(x, w, window_strides=(1, 1), padding=[(padding, padding), (padding, padding)], dimension_numbers=('NCHW', 'OIHW', 'NCHW'))

        def group_norm(x, gamma, beta):
            B, C, H, W = x.shape
            xg = x.reshape(B, GROUPS, C // GROUPS, H, W)
            mean = xg.mean(axis=(2, 3, 4), keepdims=True)
            var = xg.var(axis=(2, 3, 4), keepdims=True)
            xn = ((xg - mean) * lax.rsqrt(var + EPS)).reshape(B, C, H, W)
            return xn * gamma[None, :, None, None] + beta[None, :, None, None]

        def top_pool(x):
            return lax.cummax(x, axis=2, reverse=True)

        def left_pool(x):
            return lax.cummax(x, axis=3, reverse=True)
        p1 = jax.nn.relu(conv2d(x, p1_w, 1) + p1_b[None, :, None, None])
        pool1 = top_pool(p1)
        p2 = jax.nn.relu(conv2d(x, p2_w, 1) + p2_b[None, :, None, None])
        pool2 = left_pool(p2)
        p_gn1 = group_norm(conv2d(pool1 + pool2, p_w, 1), p_gn_g, p_gn_b)
        gn1 = group_norm(conv2d(x, c1_w, 0), gn1_g, gn1_b)
        relu1 = jax.nn.relu(p_gn1 + gn1)
        out = jax.nn.relu(conv2d(relu1, c2_w, 1) + c2_b[None, :, None, None])
        return out

    def _gn(v, G=32, eps=1e-05):
        B_, C_, H_, W_ = v.shape
        g = v.reshape(B_, G, C_ // G, H_, W_)
        m = jnp.mean(g, axis=(2, 3, 4), keepdims=True)
        s = jnp.var(g, axis=(2, 3, 4), keepdims=True)
        return ((g - m) / jnp.sqrt(s + eps)).reshape(v.shape)

    def _ln_c(v, eps=1e-06):
        m = jnp.mean(v, axis=1, keepdims=True)
        s = jnp.var(v, axis=1, keepdims=True)
        return (v - m) / jnp.sqrt(s + eps)

    def _ln_t(v, eps=1e-05):
        m = jnp.mean(v, axis=-1, keepdims=True)
        s = jnp.var(v, axis=-1, keepdims=True)
        return (v - m) / jnp.sqrt(s + eps)

    def _to_tokens(v):
        B_, C_, H_, W_ = v.shape
        return v.reshape(B_, C_, H_ * W_).transpose(0, 2, 1)

    def _from_tokens(t, like):
        B_, C_, H_, W_ = like.shape
        return t.transpose(0, 2, 1).reshape(B_, C_, H_, W_)
    x = x + _L0_conv_ref(_gn(x), L0_conv_Wq, L0_conv_Wk, L0_conv_Wv, L0_conv_off_w, L0_conv_off_b, L0_conv_attn_w, L0_conv_attn_b, L0_conv_Wo)
    x = x + _L1_conv_ref(_gn(x), L1_conv_p1_w, L1_conv_p1_b, L1_conv_p2_w, L1_conv_p2_b, L1_conv_p_w, L1_conv_p_gn_g, L1_conv_p_gn_b, L1_conv_c1_w, L1_conv_gn1_g, L1_conv_gn1_b, L1_conv_c2_w, L1_conv_c2_b)
    return x

_drawn_inputs = setup_inputs


def setup_inputs(seed=0):
    import zlib

    import numpy as np

    out = dict(_drawn_inputs(seed))
    spreads = {'L0_conv_off_b': (0.0, 0.1),
     'L0_conv_attn_b': (0.0, 0.8),
     'L1_conv_p1_b': (0.0, 0.481),
     'L1_conv_p2_b': (0.0, 0.746),
     'L1_conv_p_gn_g': (1.0, 0.2),
     'L1_conv_p_gn_b': (0.0, 0.277),
     'L1_conv_gn1_g': (1.0, 0.2),
     'L1_conv_gn1_b': (0.0, 0.1),
     'L1_conv_c2_b': (0.0, 0.1)}
    factors = {'L0_conv_attn_w': 3.18}
    for name, (base, spread) in spreads.items():
        noise = np.random.default_rng([zlib.crc32(name.encode()), seed]).standard_normal(out[name].shape)
        drawn = base * np.exp(spread * noise) if base else spread * noise
        out[name] = jnp.asarray(drawn.astype(out[name].dtype))
    for name, factor in factors.items():
        out[name] = (out[name] * factor).astype(out[name].dtype)
    return out
```

```python
from contextlib import ExitStack

import numpy as np

import concourse.bass as bass
from concourse import mybir

ALU = mybir.AluOpType
ACT = mybir.ActivationFunctionType
F32 = mybir.dt.float32
I32 = mybir.dt.int32
AX_X = mybir.AxisListType.X

N, C, H, W = 8, 64, 16, 16
HEADS, KS = 8, 3
K2 = KS * KS
HD = C // HEADS
CD = 32
P = 128
HALF = N // 2
HW = H * W
PW = W + 2
NCH = 3 * K2 * HEADS
KHW = K2 * HEADS * W
EPS = 1e-5
STEP = 0.5 * (W - 1) * (2.0 / W)
XC = 4
CHUNKS = W // XC
CK = K2 * XC * HEADS
CX = XC * HEADS
CV = XC * C
WIN = 2
ND = 2 * WIN + 1
PADX = W - 1
VW = W + 2 * PADX
DYS = range(-WIN, WIN + 1)
FULL = 2 * (W - 1) + 1
DX = {dy: (1 if abs(dy) == WIN else WIN) for dy in DYS}

C_ID = 0
C_SH = P
C_GB = C_SH + 4 * P
C_GT = C_GB + P
C_RAMP = C_GT + 2 * P
NCONST = C_RAMP + 2 * W - 1

FAR_ROWS = [(0, PADX - WIN, [(0, FULL)]),
            (PADX - WIN, PADX - WIN + 1, [(0, PADX - 1), (PADX + 2, FULL)]),
            (PADX - WIN + 1, PADX + WIN, [(0, PADX - WIN), (PADX + WIN + 1, FULL)]),
            (PADX + WIN, PADX + WIN + 1, [(0, PADX - 1), (PADX + 2, FULL)]),
            (PADX + WIN + 1, FULL, [(0, FULL)])]


def shape_constants():
    c = np.zeros((P, NCONST), np.float32)
    i = np.arange(P)
    c[i, C_ID + i] = 1
    for s, dy in enumerate((-2, -1, 1, 2)):
        rows = i[(i + N * dy >= 0) & (i + N * dy < P)]
        c[rows + N * dy, C_SH + s * P + rows] = 1
    same_group = (i[:, None] % C) // 2 == (i[None, :] % C) // 2
    c[:, C_GB:C_GB + P] = 0.5 * (same_group & (i[:, None] // C == i[None, :] // C))
    for half in range(2):
        c[:, C_GT + half * P:C_GT + (half + 1) * P] = 0.5 * (same_group & (i[:, None] // C == half))
    c[:, C_RAMP:C_RAMP + 2 * W - 1] = np.arange(1 - W, W)
    return c


def build(nc, x, consts, w_off, w_v, off_bias, w_o, w12, b12, wp, wc1, wc2, vecs, out):
    with ExitStack() as ctx:
        def sb(name, shape, dt=F32):
            return ctx.enter_context(nc.sbuf_tensor(name, shape, dt))

        def sem(name):
            return ctx.enter_context(nc.semaphore(name))

        cst = sb("cst", [P, NCONST])
        x_b = sb("x_b", [P, HALF, HW])
        x_t = sb("x_t", [P, N, HW])
        g_t = sb("g_t", [P, PW, PW, N])
        w_off_s = sb("w_off_s", [P, 2 * KS, NCH])
        w_v_s = sb("w_v_s", [P, C])
        bias_s = sb("bias_s", [P, NCH])
        u = sb("u", [P, 3 * K2, W, HEADS])
        mod = sb("mod", [P, K2, W, HEADS])
        dist = sb("dist", [P, ND, 2, CK])
        hat = sb("hat", [P, 2, ND, 2, CK])
        wy = sb("wy", [P, 2, ND, CK])
        prod = sb("prod", [P, 2, ND, CK])
        cell = sb("cell", [P, 2, ND, CX])
        v = sb("v", [P, ND, W + 2 * WIN, C])
        part = sb("part", [P, 2, ND, CV])
        comb = sb("comb", [P, W, C])
        comb_t = sb("comb_t", [P, W // 2, P])
        w_o_s = sb("w_o_s", [P, C])
        viol = sb("viol", [P, 3, CK])
        vmax = sb("vmax", [P, CHUNKS])
        vflag = sb("vflag", [P, 1])
        vcount = sb("vcount", [1, 1], I32)
        ones = sb("ones", [P, 1])
        vfar = sb("vfar", [P, VW, C])
        hat_flat = hat[:, :, :, :, :].rearrange("p b d a s -> p (b d a s)")
        fdist = hat_flat[:, 0:2 * KHW].rearrange("p (a k q) -> p a k q", a=2, k=K2)
        fprod = hat_flat[:, 2 * KHW:3 * KHW].rearrange("p (k q) -> p k q", k=K2)
        fmove = sb("fmove", [P, 1])
        fcell = sb("fcell", [P, CX * CHUNKS])
        fpart = hat_flat[:, 3 * KHW:3 * KHW + W * C].rearrange("p (x c) -> p x c", c=C)
        x1 = sb("x1", [P, HALF, HW])
        g1 = sb("g1", [P, HALF, PW, PW])
        w12_s = sb("w12_s", [P, K2, P])
        wp_s = sb("wp_s", [P, K2, P])
        wc1_s = sb("wc1_s", [P, P])
        wc2_s = sb("wc2_s", [P, K2, P])
        vec_s = sb("vec_s", [P, 5])
        b12_s = sb("b12_s", [P, 1])
        r12 = x_t[:, 0:HALF, :].rearrange("p n (y x) -> p n y x", x=W)
        pool_a = x_t[:, HALF:N, :].rearrange("p n (y x) -> p n y x", x=W)
        pooled = sb("pooled", [P, HALF, PW, PW])
        c_aff = x_b
        pre = comb_t[:, :, :].rearrange("p j q -> p (j q)").rearrange("p (n q) -> p n q", q=HW)
        g2 = sb("g2", [P, HALF, PW, PW])
        res = sb("res", [P, HALF, HW])
        bn = sb("bn", [P, 4, HALF, 6])
        mv = sb("mv", [P, 4, HALF, 2])
        sq = sb("sq", [P, 4, N])
        ab = sb("ab", [P, 4, 4, N])
        half_pow = sb("half_pow", [P, N])

        bank = [ctx.enter_context(nc.psum_tensor(f"bank{i}", [P, 512], F32)) for i in range(8)]

        ld_x = [sem(f"ld_x{i}") for i in range(2)]
        ld_xt = [sem(f"ld_xt{i}") for i in range(2)]
        ld_cst = sem("ld_cst")
        ld_w0 = [sem(f"ld_w0_{i}") for i in range(4)]
        ld_w1 = [sem(f"ld_w1_{i}") for i in range(10)]
        zeroed = sem("zeroed")
        step = sem("step")
        norm_ready = sem("norm_ready")
        stats_in = sem("stats_in")
        stats_ps = sem("stats_ps")
        var_ready = sem("var_ready")
        rstd_ready = sem("rstd_ready")
        g_ready = sem("g_ready")
        v_ps = sem("v_ps")
        v_ready = sem("v_ready")
        off_ps = sem("off_ps")
        u_ready = sem("u_ready")
        mod_ready = sem("mod_ready")
        dist_done = sem("dist_done")
        hat_ready = sem("hat_ready")
        dist_read = sem("dist_read")
        hat_used = sem("hat_used")
        part_ready = sem("part_ready")
        part_used = sem("part_used")
        flag_in = sem("flag_in")
        flag_ps = sem("flag_ps")
        flag_sb = sem("flag_sb")
        comb_part = sem("comb_part")
        comb_ready = sem("comb_ready")
        comb_tp = sem("comb_tp")
        comb_ts = sem("comb_ts")
        y0_ps = sem("y0_ps")
        g1_ready = sem("g1_ready")
        r12_ps = sem("r12_ps")
        c_ps = sem("c_ps")
        r12_ready = sem("r12_ready")
        pooled_ready = sem("pooled_ready")
        p_ps = sem("p_ps")
        caff_ready = sem("caff_ready")
        pre_ready = sem("pre_ready")
        g2_ready = sem("g2_ready")
        o_ps = sem("o_ps")
        relu_ready = sem("relu_ready")
        res_ready = sem("res_ready")
        stored = sem("stored")
        far_v0 = sem("far_v0")
        far_v = sem("far_v")
        far_row_done = sem("far_row_done")
        far_runs = sem("far_runs")
        far = sem("far")

        v_dram = nc.dram_tensor("v_rows", [P + 2 * (H - 1) * N, W * C], F32, kind="Internal").ap()

        block = ctx.enter_context(nc.Block())

        x_d = x.rearrange("n c h w -> n c (h w)")
        out_d = out.rearrange("n c h w -> n c (h w)")
        lo, hi = slice(0, C), slice(C, P)

        @block.sync
        def _(sp):
            for half in range(2):
                sp.dma_start(x_b[half * C:(half + 1) * C, :, :],
                             x_d[half * HALF:(half + 1) * HALF].rearrange("n c p -> c n p")).then_inc(ld_x[half], 16)
            sp.dma_start(x_t[lo, :, :], x_d.rearrange("n c p -> c n p")).then_inc(ld_xt[0], 16)
            sp.dma_start(w_v_s[:, :], w_v).then_inc(ld_w0[0], 16)
            sp.dma_start(w_off_s[:, :, :], w_off).then_inc(ld_w0[1], 16)
            sp.dma_start(w_o_s[:, :], w_o).then_inc(ld_w0[3], 16)
            sp.wait_ge(zeroed, 2)
            for b in range(2):
                for half in range(2):
                    cols = slice(b * C + half * CD, b * C + (half + 1) * CD)
                    sp.dma_start(w12_s[half * C:(half + 1) * C, :, cols], w12[b]).then_inc(ld_w1[2 * b + half], 16)
            for b in range(2):
                for half in range(2):
                    rows = slice(b * C + half * CD, b * C + (half + 1) * CD)
                    sp.dma_start(wp_s[rows, :, half * C:(half + 1) * C], wp).then_inc(ld_w1[4 + 2 * b + half], 16)
            sp.wait_ge(flag_sb, 1)
            sp.wait_ge(v_ready, ND)
            count = sp.value_load(vcount[0:1, 0:1], min_val=0, max_val=P)
            with sp.If(count > 0):
                sp.wait_ge(far_row_done, 1)
                pad = (H - 1) * N
                flat = vfar[:, 0:W, :].rearrange("p x c -> p (x c)")
                sp.dma_start(v_dram[0:pad, :], flat[0:pad, :]).then_inc(far_v0, 16)
                sp.dma_start(v_dram[pad + P:, :], flat[0:pad, :]).then_inc(far_v0, 16)
                sp.dma_start(v_dram[pad:pad + P, :],
                             v[:, WIN, WIN:WIN + W, :].rearrange("p x c -> p (x c)")).then_inc(far_v0, 16)
                sp.wait_ge(far_v0, 48)
                with sp.Fori(0, FULL) as k:
                    sp.wait_ge(far_row_done, k + 1)
                    sp.dma_start(vfar[:, PADX:PADX + W, :].rearrange("p x c -> p (x c)"),
                                 v_dram[bass.ds(k * N, P), :]).then_inc(far_v, 16)
            for j in range(2):
                sp.wait_ge(res_ready, j + 1)
                for half in range(2):
                    n0 = half * HALF + 2 * j
                    sp.dma_start(out_d[n0:n0 + 2].rearrange("n c p -> c n p"),
                                 res[half * C:(half + 1) * C, 2 * j:2 * j + 2, :]).then_inc(stored, 16)
            sp.wait_ge(stored, 64)

        @block.gpsimd
        def _(pool):
            nc.gpsimd.memset(g_t[:, :, :, :], 0.0).then_inc(zeroed, 1)
            nc.gpsimd.memset(half_pow[:, :], -0.5)
            nc.gpsimd.memset(ones[:, :], 1.0)
            nc.gpsimd.memset(w12_s[:, :, :], 0.0)
            nc.gpsimd.memset(wp_s[:, :, :], 0.0)
            nc.gpsimd.memset(wc1_s[:, :], 0.0)
            nc.gpsimd.memset(wc2_s[:, :, :], 0.0).then_inc(zeroed, 1)
            pool.wait_ge(zeroed, 2)
            for s, cols in enumerate((N, HALF, HALF, HALF)):
                pool.wait_ge(var_ready, s + 1)
                nc.gpsimd.tensor_tensor(ab[:, s, 2, 0:cols], ab[:, s, 1, 0:cols], half_pow[:, 0:cols],
                                        ALU.pow).then_inc(rstd_ready, 1)
                if s == 0:
                    nc.gpsimd.memset(v[:, :, :, :], 0.0).then_inc(zeroed, 1)
                    nc.gpsimd.memset(g1[:, :, :, :], 0.0)
                    nc.gpsimd.memset(pooled[:, :, :, :], 0.0)
                    nc.gpsimd.memset(g2[:, :, :, :], 0.0).then_inc(zeroed, 1)

        def gview(tile, n0, n, half=slice(0, P)):
            return tile[half, n0:n0 + n, 1:H + 1, 1:W + 1]

        @block.scalar
        def _(act):
            act.dma_start(cst[:, :], consts).then_inc(ld_cst, 16)
            act.dma_start(x_t[hi, :, :], x_d.rearrange("n c p -> c n p")).then_inc(ld_xt[1], 16)
            act.dma_start(bias_s[:, :], off_bias.to_broadcast([P, NCH])).then_inc(ld_w0[2], 16)
            act.dma_start(vec_s[:, :], vecs).then_inc(ld_w1[8], 16)
            act.dma_start(b12_s[:, :], b12).then_inc(ld_w1[8], 16)
            act.wait_ge(zeroed, 2)
            for half in range(2):
                rows = slice(half * C, (half + 1) * C)
                act.dma_start(wc1_s[rows, rows], wc1).then_inc(ld_w1[9], 16)
                act.dma_start(wc2_s[rows, :, rows], wc2).then_inc(ld_w1[9], 16)
            act.wait_ge(ld_xt[1], 16)
            act.wait_ge(norm_ready, 1)
            for n in range(N):
                nc.scalar.activation(g_t[hi, 0:W, 1:H + 1, n].rearrange("p x y -> p y x"), x_t[hi, n, :].rearrange("p (y x) -> p y x", x=W),
                                     ACT.Identity, bias=ab[hi, 0, 3, n:n + 1],
                                     scale=ab[hi, 0, 2, n:n + 1]).then_inc(g_ready, 1)
            act.wait_ge(zeroed, 3)
            for s, dy in enumerate((0, -2, -1, 1, 2)):
                act.wait_ge(v_ps, s + 1)
                for b in range(2):
                    bk = bank[4 + 2 * (s % 2) + b]
                    last = nc.scalar.activation(v[:, WIN + dy, WIN + b * W // 2:WIN + (b + 1) * W // 2, :],
                                                bk[:, :].rearrange("p (x c) -> p x c", c=C), ACT.Copy)
                last.then_inc(v_ready, 1)

            def evacuate(c):
                act.wait_ge(part_used, ND * (c + 1))
                nc.scalar.activation(comb[:, c * XC:(c + 1) * XC, :],
                                     bank[4 + c][:, 0:CV].rearrange("p (x c) -> p x c", c=C),
                                     ACT.Copy).then_inc(comb_part, 1)

            for c in range(CHUNKS):
                xs = slice(c * XC, (c + 1) * XC)
                act.wait_ge(u_ready, c + 1)
                nc.scalar.activation(mod[:, :, xs, :], u[:, 2 * K2:, xs, :], ACT.Sigmoid).then_inc(mod_ready, 1)
                if c:
                    act.wait_ge(hat_ready, c)
                    act.wait_ge(dist_read, c)
                for d in range(ND):
                    for a in range(2):
                        last = nc.scalar.activation(
                            dist[:, d, a, :].rearrange("p (k x h) -> p k x h", x=XC, h=HEADS),
                            u[:, a * K2:(a + 1) * K2, xs, :], ACT.Abs, bias=float(WIN - d), scale=STEP)
                last.then_inc(dist_done, 1)
                act.wait_ge(dist_done, c + 1)
                if c >= 2:
                    act.wait_ge(hat_used, ND * (c - 1))
                nc.scalar.activation(hat[:, c % 2], dist[:, :, :, :], ACT.Relu, bias=1.0,
                                     scale=-1.0).then_inc(hat_ready, 1)
                if c:
                    evacuate(c - 1)
            evacuate(CHUNKS - 1)

            for b in range(2):
                act.wait_ge(comb_tp, b + 1)
                nc.scalar.activation(comb_t[:, b * W // 4:(b + 1) * W // 4, :],
                                     bank[b][:, :].rearrange("p (j q) -> p j q", q=P), ACT.Copy).then_inc(comb_ts, 1)

            act.wait_ge(zeroed, 4)
            act.wait_ge(norm_ready, 2)
            for n in range(HALF):
                nc.scalar.activation(gview(g1, n, 1), x1[:, n:n + 1, :].rearrange("p n (y x) -> p n y x", x=W),
                                     ACT.Identity, bias=ab[:, 1, 3, n:n + 1],
                                     scale=ab[:, 1, 2, n:n + 1]).then_inc(g1_ready, 1)
            act.wait_ge(ld_w1[8], 32)
            for b in range(2):
                act.wait_ge(r12_ps, b + 1)
                nc.scalar.activation(r12[:, 2 * b:2 * b + 2, :, :],
                                     bank[b][:, :].rearrange("p (n y x) -> p n y x", n=2, x=W), ACT.Relu,
                                     bias=b12_s[:, 0:1]).then_inc(r12_ready, 1)
            act.wait_ge(norm_ready, 3)
            for n in range(HALF):
                last = nc.scalar.activation(c_aff[:, n, :], bank[2 + n // 2][:, (n % 2) * HW:(n % 2 + 1) * HW],
                                            ACT.Identity, bias=ab[:, 2, 3, n:n + 1], scale=ab[:, 2, 2, n:n + 1])
            last.then_inc(caff_ready, 1)
            for n in range(HALF):
                act.wait_ge(pre_ready, n + 1)
                nc.scalar.activation(gview(g2, n, 1), pre[:, n:n + 1, :].rearrange("p n (y x) -> p n y x", x=W),
                                     ACT.Relu, bias=ab[:, 3, 3, n:n + 1]).then_inc(g2_ready, 1)
            for b in range(2):
                act.wait_ge(o_ps, b + 1)
                nc.scalar.activation(res[:, 2 * b:2 * b + 2, :], bank[6 + b][:, :].rearrange("p (n q) -> p n q", n=2),
                                     ACT.Relu, bias=vec_s[:, 4:5]).then_inc(relu_ready, 1)

        @block.vector
        def _(ve):
            chain = [0]

            def link(ins):
                chain[0] += 1
                ins.then_inc(step, 1)
                ve.wait_ge(step, chain[0])

            def norm_stats(s, views):
                for n, view in enumerate(views):
                    last = nc.vector.bn_stats(bn[:, s, n, :], view)
                link(last)
                for n in range(HALF):
                    last = nc.vector.bn_aggr(mv[:, s, n, :], bn[:, s, n, :])
                link(last)
                link(nc.vector.tensor_tensor(sq[:, s, 0:HALF], mv[:, s, :, 0], mv[:, s, :, 0], ALU.mult))
                nc.vector.tensor_tensor(mv[:, s, :, 1], mv[:, s, :, 1], sq[:, s, 0:HALF],
                                        ALU.add).then_inc(stats_in, 1)

            def norm_params(s, cols, stat_bank, gamma=None, beta=None, extra=None):
                ve.wait_ge(stats_ps, s + 1)
                link(nc.vector.tensor_copy(ab[:, s, 0:2, 0:cols], stat_bank[:, 0:2 * cols].rearrange("p (n t) -> p t n", t=2)))
                link(nc.vector.tensor_tensor(sq[:, s, 0:cols], ab[:, s, 0, 0:cols], ab[:, s, 0, 0:cols], ALU.mult))
                nc.vector.scalar_tensor_tensor(ab[:, s, 1, 0:cols], ab[:, s, 1, 0:cols], EPS, sq[:, s, 0:cols],
                                               ALU.add, ALU.subtract).then_inc(var_ready, 1)
                ve.wait_ge(rstd_ready, s + 1)
                if gamma is not None:
                    link(nc.vector.tensor_scalar(ab[:, s, 2, 0:cols], ab[:, s, 2, 0:cols], gamma, None, ALU.mult))
                ins = nc.vector.scalar_tensor_tensor(ab[:, s, 3, 0:cols], ab[:, s, 0, 0:cols], -1.0,
                                                     ab[:, s, 2, 0:cols], ALU.mult, ALU.mult)
                if beta is not None:
                    link(ins)
                    ins = nc.vector.tensor_scalar(ab[:, s, 3, 0:cols], ab[:, s, 3, 0:cols], beta, None, ALU.add)
                if extra is not None:
                    link(ins)
                    ins = nc.vector.tensor_scalar(ab[:, s, 3, 0:cols], ab[:, s, 3, 0:cols], extra, None, ALU.add)
                ins.then_inc(norm_ready, 1)
                ve.wait_ge(norm_ready, s + 1)

            def far_displacements(ve):
                def wait(n):
                    ve.wait_ge(far, n)

                def run(base, steps):
                    for j, ins in enumerate(steps):
                        ins().then_inc(far, 1)
                        wait(base + j + 1)
                    ve.sem_inc(far_runs, 1)
                    return base + len(steps)

                ux = u[:, 0:K2, :, :].rearrange("p k x h -> p k (x h)")
                uy = u[:, K2:2 * K2, :, :].rearrange("p k x h -> p k (x h)")
                m = mod[:, :, :, :].rearrange("p k x h -> p k (x h)")
                middle = vfar[:, PADX:PADX + W, :]

                def hat_steps(a, src, i):
                    t = fdist[:, a]
                    ramp = cst[:, bass.ds(C_RAMP + i, 1)]
                    return [lambda: nc.vector.tensor_copy(fmove[:, :], ramp),
                            lambda: nc.vector.tensor_scalar(t, src, STEP, fmove[:, 0:1], ALU.mult, ALU.subtract),
                            lambda: nc.vector.scalar_tensor_tensor(t, t, -1.0, t, ALU.mult, ALU.min),
                            lambda: nc.vector.tensor_scalar(t, t, 1.0, 0.0, ALU.add, ALU.max)]

                def row_steps(i):
                    return hat_steps(1, uy, i) + [
                        lambda: nc.vector.tensor_tensor(fdist[:, 1], fdist[:, 1], m, ALU.mult)]

                def cell_steps(i):
                    return hat_steps(0, ux, i) + [
                        lambda: nc.vector.tensor_tensor(fprod[:, :, :], fdist[:, 0], fdist[:, 1], ALU.mult),
                        lambda: nc.vector.tensor_reduce(fcell[:, :], fprod[:, :, :].rearrange("p k q -> p q k"),
                                                        AX_X, ALU.add),
                        lambda: nc.vector.tensor_tensor(
                            fpart[:, :, :].rearrange("p x (h e) -> p (x h) e", e=HD),
                            vfar[:, bass.ds(i, W), :].rearrange("p x (h e) -> p (x h) e", e=HD),
                            fcell[:, :].unsqueeze(2).to_broadcast([P, W * HEADS, HD]), ALU.mult),
                        lambda: nc.vector.tensor_tensor(comb[:, :, :], comb[:, :, :], fpart[:, :, :], ALU.add)]

                CELL = 8

                def columns(base, i0, i1):
                    with ve.Fori(i0, i1) as i:
                        run(base + (i - i0) * CELL, cell_steps(i))
                    return base + (i1 - i0) * CELL

                n = run(0, [lambda: nc.vector.memset(vfar[:, :, :], 0.0)])
                ve.sem_inc(far_row_done, 1)
                for r0, r1, ranges in FAR_ROWS:
                    per_row = 5 + sum(i1 - i0 for i0, i1 in ranges) * CELL
                    with ve.Fori(r0, r1) as k:
                        base = n + (k - r0) * per_row
                        ve.wait_ge(far_v, (k + 1) * 16)
                        base = run(base, row_steps(k))
                        for i0, i1 in ranges:
                            base = columns(base, i0, i1)
                        ve.sem_inc(far_row_done, 1)
                    n += per_row * (r1 - r0)

            for half in range(2):
                ve.wait_ge(ld_x[half], 16)
            norm_stats(0, [x_b[:, n, :] for n in range(HALF)])
            norm_params(0, N, bank[7])
            ve.wait_ge(ld_xt[0], 16)
            ve.wait_ge(zeroed, 1)
            for n in range(N):
                nc.vector.tensor_scalar(g_t[lo, 1:W + 1, 1:H + 1, n].rearrange("p x y -> p y x"), x_t[lo, n, :].rearrange("p (y x) -> p y x", x=W),
                                        ab[lo, 0, 2, n:n + 1], ab[lo, 0, 3, n:n + 1], ALU.mult,
                                        ALU.add).then_inc(g_ready, 1)
            ve.wait_ge(ld_w0[2], 16)

            def offsets(c):
                ve.wait_ge(off_ps, c + 1)
                for b in range(2):
                    x0 = c * XC + 2 * b
                    last = nc.vector.tensor_tensor(
                        u[:, :, x0:x0 + 2, :].rearrange("p k x h -> p x k h"),
                        bank[2 * (c % 2) + b][:, 0:2 * NCH].rearrange("p (x k h) -> p x k h", x=2, h=HEADS),
                        bias_s[:, :].rearrange("p (k h) -> p k h", h=HEADS).unsqueeze(1).to_broadcast(
                            [P, 2, 3 * K2, HEADS]), ALU.add)
                last.then_inc(u_ready, 1)

            def flag(c):
                a = dist[:, WIN, 0, :], dist[:, WIN, 1, :]
                nc.vector.tensor_tensor(viol[:, 0, :], a[0], a[1], ALU.max)
                link(nc.vector.tensor_tensor(viol[:, 1, :], a[0], a[1], ALU.min))
                link(nc.vector.scalar_tensor_tensor(viol[:, 2, :], viol[:, 0, :], 1.0 / WIN, viol[:, 1, :],
                                                    ALU.mult, ALU.max))
                nc.vector.tensor_reduce(vmax[:, c:c + 1], viol[:, 2, :], AX_X, ALU.max).then_inc(dist_read, 1)

            def chunk(c):
                ve.wait_ge(dist_done, c + 1)
                flag(c)
                ve.wait_ge(hat_ready, c + 1)
                ve.wait_ge(mod_ready, c + 1)
                hc = hat[:, c % 2]
                m = mod[:, :, c * XC:(c + 1) * XC, :].rearrange("p k x h -> p k (x h)")
                for d in range(ND):
                    last = nc.vector.tensor_tensor(wy[:, c % 2, d].rearrange("p (k q) -> p k q", k=K2),
                                                   hc[:, d, 1, :].rearrange("p (k q) -> p k q", k=K2), m, ALU.mult)
                link(last)

                def product(i, dy):
                    nd = 2 * DX[dy] + 1
                    d0 = WIN - DX[dy]
                    return nc.vector.tensor_tensor(
                        prod[:, i % 2, 0:nd, :], hc[:, d0:d0 + nd, 0, :],
                        wy[:, c % 2, i:i + 1, :].to_broadcast([P, nd, CK]), ALU.mult)

                def ksum(i, dy):
                    nd = 2 * DX[dy] + 1
                    return nc.vector.tensor_reduce(
                        cell[:, i % 2, 0:nd, :], prod[:, i % 2, 0:nd, :].rearrange("p d (k q) -> p d q k", k=K2),
                        AX_X, ALU.add)

                def apply(i, dy):
                    nd = 2 * DX[dy] + 1
                    n = ND * c + i
                    if n >= 2:
                        ve.wait_ge(part_used, n - 1)
                    if n < ND:
                        ve.wait_ge(v_ready, ND)
                    xa = c * XC + WIN - DX[dy]
                    v0 = v[:, i, xa:xa + XC, :]
                    moved = bass.AP(v0.tensor, v0.offset, [v0.ap[0], [C, nd], [HD, CX], [1, HD]])
                    nc.vector.tensor_tensor(
                        part[:, n % 2, 0:nd, :].rearrange("p d (q e) -> p d q e", e=HD), moved,
                        cell[:, i % 2, 0:nd, :].unsqueeze(3).to_broadcast([P, nd, CX, HD]),
                        ALU.mult).then_inc(part_ready, 1)

                for i, dy in enumerate(DYS):
                    ins = product(i, dy)
                    ins.then_inc(hat_used, 1)
                    ve.wait_ge(hat_used, ND * c + i + 1)
                    link(ksum(i, dy))
                    apply(i, dy)

            offsets(0)
            for c in range(CHUNKS):
                if c + 1 < CHUNKS:
                    offsets(c + 1)
                chunk(c)
            ve.wait_ge(dist_read, CHUNKS)
            link(nc.vector.tensor_reduce(vflag[:, :], vmax[:, :], AX_X, ALU.max))
            nc.vector.tensor_scalar(vflag[:, :], vflag[:, :], 1.0, None, ALU.is_gt).then_inc(flag_in, 1)
            ve.wait_ge(flag_ps, 1)
            nc.vector.tensor_copy(vcount[:, :], bank[3][0:1, 0:1]).then_inc(flag_sb, 1)
            ve.wait_ge(flag_sb, 1)
            ve.wait_ge(comb_part, CHUNKS)
            count = ve.value_load(vcount[0:1, 0:1], min_val=0, max_val=P)
            with ve.If(count > 0):
                far_displacements(ve)
            nc.vector.memset(vflag[:, :], 0.0).then_inc(comb_ready, 1)

            for par in range(2):
                ve.wait_ge(y0_ps, par + 1)
                def column_pairs(t):
                    return t[:, :, :].rearrange("p n (y j a) -> p a j y n", a=2, j=W // 2)[:, par]
                last = nc.vector.tensor_tensor(
                    column_pairs(x1), bank[2 + par][:, :].rearrange("p (j y n) -> p j y n", y=H, n=HALF),
                    column_pairs(x_b), ALU.add)
            link(last)
            norm_stats(1, [x1[:, n, :] for n in range(HALF)])
            norm_params(1, HALF, bank[7])

            ve.wait_ge(ld_w1[8], 32)
            for b in range(2):
                ve.wait_ge(c_ps, b + 1)
            norm_stats(2, [bank[2 + n // 2][:, (n % 2) * HW:(n % 2 + 1) * HW] for n in range(HALF)])
            for b in range(2):
                ve.wait_ge(r12_ready, b + 1)
            src, dst = r12, pool_a
            for s in (1, 2, 4, 8):
                nc.vector.tensor_tensor(dst[lo, :, 0:H - s, :].rearrange("p n y x -> p n (y x)"),
                                        src[lo, :, 0:H - s, :].rearrange("p n y x -> p n (y x)"),
                                        src[lo, :, s:H, :].rearrange("p n y x -> p n (y x)"), ALU.max)
                nc.vector.tensor_copy(dst[lo, :, H - s:H, :], src[lo, :, H - s:H, :])
                nc.vector.tensor_tensor(dst[hi, :, :, 0:W - s], src[hi, :, :, 0:W - s], src[hi, :, :, s:W], ALU.max)
                link(nc.vector.tensor_copy(dst[hi, :, :, W - s:W], src[hi, :, :, W - s:W]))
                src, dst = dst, src
            ve.wait_ge(zeroed, 4)
            nc.vector.tensor_copy(gview(pooled, 0, HALF), src[:, :, :, :]).then_inc(pooled_ready, 1)
            norm_params(2, HALF, bank[7][:, 16:32], gamma=vec_s[:, 2:3], beta=vec_s[:, 3:4],
                        extra=vec_s[:, 1:2])

            for b in range(2):
                ve.wait_ge(p_ps, b + 1)
            norm_stats(3, [bank[4 + n // 2][:, (n % 2) * HW:(n % 2 + 1) * HW] for n in range(HALF)])
            norm_params(3, HALF, bank[7][:, 32:48], gamma=vec_s[:, 0:1])
            ve.wait_ge(caff_ready, 1)
            for n in range(HALF):
                nc.vector.scalar_tensor_tensor(pre[:, n, :], bank[4 + n // 2][:, (n % 2) * HW:(n % 2 + 1) * HW],
                                               ab[:, 3, 2, n:n + 1], c_aff[:, n, :], ALU.mult,
                                               ALU.add).then_inc(pre_ready, 1)
            for b in range(2):
                ve.wait_ge(relu_ready, b + 1)
                nc.vector.tensor_tensor(res[:, 2 * b:2 * b + 2, :], res[:, 2 * b:2 * b + 2, :],
                                        x1[:, 2 * b:2 * b + 2, :], ALU.add).then_inc(res_ready, 1)

        @block.tensor
        def _(pe):
            def group_means(s, out_ap, mats):
                pe.wait_ge(stats_in, s + 1)
                for i, m in enumerate(mats):
                    last = nc.tensor.matmul(out_ap[:, 2 * HALF * i:2 * HALF * (i + 1)], cst[:, m:m + P],
                                            mv[:, s, :, :].rearrange("p n t -> p (n t)"), start=True, stop=True)
                last.then_inc(stats_ps, 1)

            pe.wait_ge(ld_cst, 16)
            group_means(0, bank[7], (C_GT, C_GT + P))

            pe.wait_ge(g_ready, 2 * N)
            pe.wait_ge(ld_w0[0], 16)
            for xx in range(W):
                last = nc.tensor.matmul(bank[4 + xx // 8][:, (xx % 8) * C:(xx % 8 + 1) * C],
                                        g_t[:, xx + 1, 1:H + 1, :].rearrange("p y n -> p (y n)"), w_v_s[:, :], start=True, stop=True)
            last.then_inc(v_ps, 1)

            def conv(c):
                if c >= 2:
                    pe.wait_ge(u_ready, c - 1)
                for j in range(XC):
                    xx = c * XC + j
                    for t in range(2 * KS):
                        ky, single = t // 2, t % 2
                        last = nc.tensor.matmul(
                            bank[2 * (c % 2) + j // 2][:, (j % 2) * NCH:(j % 2 + 1) * NCH],
                            g_t[:, xx + 2 * single, ky:ky + H, :].rearrange("p y n -> p (y n)"), w_off_s[:, t, :],
                            start=(t == 0), stop=(t == 2 * KS - 1))
                last.then_inc(off_ps, 1)

            def shift(s):
                pe.wait_ge(v_ready, max(s - 1, 1))
                for b in range(2):
                    last = nc.tensor.matmul(bank[4 + 2 * (s % 2) + b][:, :], cst[:, C_SH + (s - 1) * P:C_SH + s * P],
                                            v[:, WIN, WIN + b * W // 2:WIN + (b + 1) * W // 2, :],
                                            start=True, stop=True)
                last.then_inc(v_ps, 1)

            pe.wait_ge(ld_w0[1], 16)
            conv(0)
            for s in range(1, ND):
                shift(s)
            conv(1)
            for c in range(CHUNKS):
                if c + 2 < CHUNKS:
                    conv(c + 2)
                for i, dy in enumerate(DYS):
                    pe.wait_ge(part_ready, ND * c + i + 1)
                    if c == 0 and i == 0:
                        pe.wait_ge(v_ready, ND)
                    nd = 2 * DX[dy] + 1
                    for j in range(nd):
                        last = nc.tensor.matmul(bank[4 + c][:, 0:CV], cst[:, C_ID:C_ID + P],
                                                part[:, (ND * c + i) % 2, j, :],
                                                start=(i == 0 and j == 0), stop=(i == ND - 1 and j == nd - 1))
                    last.then_inc(part_used, 1)
            pe.wait_ge(flag_in, 1)
            nc.tensor.matmul(bank[3][0:1, 0:1], vflag[:, :], ones[:, :], start=True, stop=True).then_inc(flag_ps, 1)
            pe.wait_ge(comb_ready, 1)
            for j in range(W // 2):
                last = nc.tensor.transpose(bank[j // 4][:, (j % 4) * P:(j % 4 + 1) * P],
                                           comb[:, 2 * j:2 * j + 2, :].rearrange("p x c -> p (x c)"),
                                           cst[:, C_ID:C_ID + P])
                if j % 4 == 3:
                    last.then_inc(comb_tp, 1)
            pe.wait_ge(comb_ts, 2)
            pe.wait_ge(ld_w0[3], 16)
            for par in range(2):
                rows = slice(par * C, (par + 1) * C)
                for half in range(2):
                    last = nc.tensor.matmul(bank[2 + par][half * C:(half + 1) * C, :], w_o_s[rows, :],
                                            comb_t[rows, :, :].rearrange("p j (y n) -> p j y n", n=N)[
                                                :, :, :, half * HALF:(half + 1) * HALF], start=True, stop=True)
                last.then_inc(y0_ps, 1)

            group_means(1, bank[7], (C_GB,))
            for i in range(8):
                pe.wait_ge(ld_w1[i], 16)
            pe.wait_ge(ld_w1[9], 64)
            pe.wait_ge(g1_ready, HALF)

            def conv3(tile, w, bk, done_sem, waits=None):
                for b in range(2):
                    if waits:
                        waits(b)
                    for t in range(K2):
                        ky, kx = t // KS, t % KS
                        last = nc.tensor.matmul(bk[b][:, :].rearrange("p (n y x) -> p n y x", n=2, x=W), w[:, t, :],
                                                tile[:, 2 * b:2 * b + 2, ky:ky + H, kx:kx + W],
                                                start=(t == 0), stop=(t == K2 - 1))
                    last.then_inc(done_sem, 1)

            for b in range(2):
                nc.tensor.matmul(bank[2 + b][:, :].rearrange("p (n y x) -> p n y x", n=2, x=W), wc1_s[:, :],
                                 g1[:, 2 * b:2 * b + 2, 1:H + 1, 1:W + 1], start=True, stop=True).then_inc(c_ps, 1)
            conv3(g1, w12_s, (bank[0], bank[1]), r12_ps)
            group_means(2, bank[7][:, 16:32], (C_GB,))
            pe.wait_ge(pooled_ready, 1)
            conv3(pooled, wp_s, (bank[4], bank[5]), p_ps)
            group_means(3, bank[7][:, 32:48], (C_GB,))
            conv3(g2, wc2_s, (bank[6], bank[7]), o_ps, lambda b: pe.wait_ge(g2_ready, 2 * b + 2))


_LAYOUT = ("x", "consts", "w_off", "w_v", "off_bias", "w_o", "w12", "b12", "wp", "wc1", "wc2", "vecs")


def kernel(**inputs):
    import numpy as _np
    import concourse.bacc as _bacc
    from concourse import mybir as _mybir
    from concourse.bass_utils import run_bass_kernel_spmd as _run

    a = {k: _np.asarray(v) for k, v in inputs.items()}
    l0 = {k[8:]: v for k, v in a.items() if k.startswith("L0_conv_")}
    l1 = {k[8:]: v for k, v in a.items() if k.startswith("L1_conv_")}
    z = _np.zeros

    def by_tap(off, attn):
        off = off.reshape((HEADS, K2, 2) + off.shape[1:])
        attn = attn.reshape((1, HEADS, K2) + attn.shape[1:])
        both = _np.concatenate([_np.moveaxis(off, 2, 0), attn])
        return _np.swapaxes(both, 1, 2).reshape((NCH,) + attn.shape[3:])

    w = by_tap(l0["off_w"], l0["attn_w"]).transpose(1, 2, 3, 0)
    w_off = z((P, 2 * KS, NCH), _np.float32)
    w_off[:C, 0::2] = w[:, :, 0]
    w_off[C:, 0::2] = w[:, :, 1]
    w_off[:C, 1::2] = w[:, :, 2]
    w_v = z((P, C), _np.float32)
    w_v[:C] = l0["Wv"].T
    taps = lambda t: t.transpose(1, 2, 3, 0).reshape(t.shape[1], K2, t.shape[0])
    twice = lambda t: _np.concatenate([t, t])
    arrays = {
        "x": a["x"], "consts": shape_constants(), "w_off": w_off, "w_v": w_v,
        "off_bias": by_tap(l0["off_b"], l0["attn_b"]).reshape(1, NCH),
        "w_o": twice(l0["Wo"].T),
        "w12": _np.stack([taps(l1["p1_w"]), taps(l1["p2_w"])]),
        "b12": _np.concatenate([twice(l1["p1_b"]), twice(l1["p2_b"])]).reshape(P, 1),
        "wp": taps(l1["p_w"]), "wc1": l1["c1_w"][:, :, 0, 0].T, "wc2": taps(l1["c2_w"]),
        "vecs": _np.stack([twice(l1[k]) for k in ("p_gn_g", "p_gn_b", "gn1_g", "gn1_b", "c2_b")], 1),
    }
    nc = _bacc.Bacc("TRN2", target_bir_lowering=False, num_devices=1)
    feed, args = {}, []
    for name in _LAYOUT:
        t = _np.ascontiguousarray(arrays[name])
        feed[f"in_{name}"] = t
        args.append(nc.dram_tensor(f"in_{name}", t.shape, _mybir.dt.from_np(t.dtype), kind="ExternalInput").ap())
    args.append(nc.dram_tensor("out_0", (N, C, H, W), F32, kind="ExternalOutput").ap())
    build(nc, *args)
    return _run(nc, [feed], core_ids=[0]).results[0]["out_0"]
```

```python
from contextlib import ExitStack

import numpy as np

import concourse.bass as bass
from concourse import mybir

ALU = mybir.AluOpType
ACT = mybir.ActivationFunctionType
F32 = mybir.dt.float32
I32 = mybir.dt.int32
AX_X = mybir.AxisListType.X

N, C, H, W = 8, 64, 16, 16
HEADS, KS = 8, 3
K2 = KS * KS
HD = C // HEADS
CD = 32
P = 128
HALF = N // 2
DUO = 2
HW = H * W
PW = W + 2
NCH = 3 * K2 * HEADS
KHW = K2 * HEADS * W
EPS = 1e-5
STEP = 0.5 * (W - 1) * (2.0 / W)
CHUNKS = ((0, 2), (2, 4), (6, 4), (10, 4), (14, 2))
NC = len(CHUNKS)
XM = 4
CKM = K2 * XM * HEADS
CXM = XM * HEADS
CVM = XM * C
WIN = 2
ND = 2 * WIN + 1
PADX = W - 1
VW = W + 2 * PADX
FULL = 2 * (W - 1) + 1
DX = [1, 2, 2, 2, 1]
PE_ROWS = (1, 3)
APPLY = (2, 1, 0, 3, 4)
PROD_SLOT = {1: 0, 3: 1, 2: 2, 0: 3, 4: 2}
PARTS = 3

FAR_ROWS = [(0, PADX - WIN, [(0, FULL)]),
            (PADX - WIN, PADX - WIN + 1, [(0, PADX - 1), (PADX + 2, FULL)]),
            (PADX - WIN + 1, PADX + WIN, [(0, PADX - WIN), (PADX + WIN + 1, FULL)]),
            (PADX + WIN, PADX + WIN + 1, [(0, PADX - 1), (PADX + 2, FULL)]),
            (PADX + WIN + 1, FULL, [(0, FULL)])]

G0, G_IN, G_C1, G_P, NORMS = 0, 1, 3, 5, 7

C_GB = 0
C_GT = C_GB + P
C_RAMP = C_GT + 2 * P
C_ID = C_RAMP + 2 * W - 1
NCONST = C_ID + P


def shape_constants():
    c = np.zeros((P, NCONST), np.float32)
    i = np.arange(P)
    c[i, C_ID + i] = 1
    same_group = (i[:, None] % C) // 2 == (i[None, :] % C) // 2
    c[:, C_GB:C_GB + P] = 0.5 * (same_group & (i[:, None] // C == i[None, :] // C))
    for half in range(2):
        c[:, C_GT + half * P:C_GT + (half + 1) * P] = 0.5 * (same_group & (i[:, None] // C == half))
    c[:, C_RAMP:C_RAMP + 2 * W - 1] = np.arange(1 - W, W)
    return c


def build(nc, x, consts, w_off, w_v, off_bias, w_o, w12, b12, wp, wc1, wc2, vecs, out):
    with ExitStack() as ctx:
        def sb(name, shape, dt=F32):
            return ctx.enter_context(nc.sbuf_tensor(name, shape, dt))

        def sem(name):
            return ctx.enter_context(nc.semaphore(name))

        cst = sb("cst", [P, NCONST])
        x_b = sb("x_b", [P, HALF, HW])
        x_t = sb("x_t", [P, N, HW])
        g_t = sb("g_t", [P, PW, PW, N])
        w_off_s = sb("w_off_s", [P, 2 * KS, NCH])
        w_v_s = sb("w_v_s", [P, P])
        bias_s = sb("bias_s", [P, NCH])
        u = sb("u", [P, 3 * K2, W, HEADS])
        mod = sb("mod", [P, K2, W, HEADS])
        dist = sb("dist", [P, ND, 2 * CKM])
        hat = sb("hat", [P, 2, ND, 2 * CKM])
        wy = sb("wy", [P, ND, CKM])
        prod = sb("prod", [P, 4, ND, CKM])
        cell = sb("cell", [P, 2, ND, CXM])
        v = sb("v", [P, ND, W + 2 * WIN, C])
        part = sb("part", [P, PARTS, ND, CVM])
        comb_t = sb("comb_t", [P, W // 2, P])
        w_o_s = sb("w_o_s", [P, C])
        edge = sb("edge", [P, CKM])
        vmin = sb("vmin", [P, NC])
        vfar_sum = sb("vfar_sum", [P, NC])
        vflag = sb("vflag", [P, 2, NC])
        vtotal = sb("vtotal", [1, 1])
        vcount = sb("vcount", [1, 1], I32)
        ones = sb("ones", [P, 1])
        warm = sb("warm", [P, 1])
        vfar = sb("vfar", [P, VW, C])
        fmove = sb("fmove", [P, 1])
        fcell = sb("fcell", [P, W * HEADS])
        hat_flat = hat[:, :, :, :].rearrange("p b d s -> p (b d s)")
        fdist = hat_flat[:, 0:2 * KHW].rearrange("p (a k q) -> p a k q", a=2, k=K2)
        fprod = hat_flat[:, 2 * KHW:3 * KHW].rearrange("p (k q) -> p k q", k=K2)
        fpart = hat_flat[:, 3 * KHW:3 * KHW + W * C].rearrange("p (x c) -> p x c", c=C)
        prod_flat = prod[:, :, :, :].rearrange("p b d s -> p (b d s)")
        far_sum = prod_flat[:, 0:W * C].rearrange("p (x c) -> p x c", c=C)
        far_t = prod_flat[:, W * C:2 * W * C].rearrange("p (j q) -> p j q", q=P)
        x1 = sb("x1", [P, HALF, HW])
        g1 = sb("g1", [P, HALF, PW, PW])
        w12_s = sb("w12_s", [P, K2, P])
        wp_s = sb("wp_s", [P, 2 * KS, P])
        wc1_s = sb("wc1_s", [P, P])
        wc2_s = sb("wc2_s", [P, K2, P])
        vec_s = sb("vec_s", [P, 5])
        b12_s = sb("b12_s", [P, 1])
        keep = sb("keep", [C, 2 * DUO * HW])
        r12 = x_t[0:C, 0:HALF, :].rearrange("p (b n) q -> p b n q", b=2)
        maxima = x_t[0:C, HALF:N, :].rearrange("p (b n) q -> p b n q", b=2)
        pooled = sb("pooled", [P, HALF, PW, PW])
        c_aff = x_b
        pre = comb_t[:, :, :].rearrange("p j q -> p (j q)").rearrange("p (n q) -> p n q", q=HW)
        g2 = sb("g2", [P, HALF, PW, PW])
        res = u[:, :, :, :].rearrange("p k x h -> p (k x h)")[:, 0:HALF * HW].rearrange("p (n q) -> p n q", q=HW)
        bn = sb("bn", [P, NORMS, HALF, 6])
        mv = sb("mv", [P, NORMS, HALF, 2])
        sq = sb("sq", [P, NORMS, N])
        ab = sb("ab", [P, NORMS, 4, N])
        half_pow = sb("half_pow", [P, N])

        bank = [ctx.enter_context(nc.psum_tensor(f"bank{i}", [P, 512], F32)) for i in range(8)]
        comb_bank, cell_bank, y0_banks = bank[4], bank[5], bank[6:8]

        ld_x = [sem(f"ld_x{i}") for i in range(2)]
        ld_xt = [sem(f"ld_xt{i}") for i in range(2)]
        ld_cst = sem("ld_cst")
        ld_w0 = [sem(f"ld_w0_{i}") for i in range(4)]
        ld_w12, ld_wp, ld_vec, ld_c = sem("ld_w12"), sem("ld_wp"), sem("ld_vec"), sem("ld_c")
        zeroed = sem("zeroed")
        v_zero = sem("v_zero")
        step = sem("step")
        stats_in = sem("stats_in")
        stats_ps = sem("stats_ps")
        var_ready = sem("var_ready")
        rstd_ready = sem("rstd_ready")
        norm_ready = sem("norm_ready")
        g_ready = sem("g_ready")
        v_ps = sem("v_ps")
        v_ready = sem("v_ready")
        v_moved = [sem(f"v_moved{i}") for i in range(ND)]
        off_ps = sem("off_ps")
        u_ready = sem("u_ready")
        mod_ready = sem("mod_ready")
        dist_done = sem("dist_done")
        far_test = sem("far_test")
        hat_ready = sem("hat_ready")
        hat_used = sem("hat_used")
        prod_ready = sem("prod_ready")
        cell_ps = sem("cell_ps")
        part_ready = sem("part_ready")
        part_used = sem("part_used")
        flag_in = sem("flag_in")
        flag_ps = sem("flag_ps")
        flag_sb = sem("flag_sb")
        comb_ts = sem("comb_ts")
        y0_ps = sem("y0_ps")
        x1_ready = sem("x1_ready")
        g1_ready = sem("g1_ready")
        r12_ps = sem("r12_ps")
        c_ps = sem("c_ps")
        r12_ready = sem("r12_ready")
        r12_used = sem("r12_used")
        pooled_ready = sem("pooled_ready")
        p_ps = sem("p_ps")
        caff_ready = sem("caff_ready")
        pre_ready = sem("pre_ready")
        g2_ready = sem("g2_ready")
        o_ps = sem("o_ps")
        relu_ready = sem("relu_ready")
        res_ready = sem("res_ready")
        stored = sem("stored")
        far_v0 = sem("far_v0")
        far_v = sem("far_v")
        far_row_done = sem("far_row_done")
        far_runs = sem("far_runs")
        far = sem("far")
        far_tp = sem("far_tp")
        far_ts = sem("far_ts")
        far_y = sem("far_y")
        far_added = sem("far_added")

        v_dram = nc.dram_tensor("v_rows", [P + 2 * (H - 1) * N, W * C], F32, kind="Internal").ap()

        block = ctx.enter_context(nc.Block())

        x_d = x.rearrange("n c h w -> n c (h w)")
        out_d = out.rearrange("n c h w -> n c (h w)")
        lo, hi = slice(0, C), slice(C, P)

        def inner(tile, n0, n, part=slice(0, P)):
            return tile[part, n0:n0 + n, 1:H + 1, 1:W + 1]

        def rows_cols(ap):
            return ap.rearrange("p (y x) -> p y x", x=W)

        def pair_stats(s):
            b = {G_IN: 5, G_IN + 1: 4, G_C1: 7, G_C1 + 1: 6, G_P: 7, G_P + 1: 7}[s]
            return bank[b][:, 0:2 * DUO]

        OUT_PARTS = ((0, DUO), (DUO, 1), (DUO + 1, 1))
        out_banks = (bank[6], bank[7], bank[0])

        @block.sync
        def _(sp):
            sp.dma_start(x_b[lo, :, :], x_d[0:HALF].rearrange("n c p -> c n p")).then_inc(ld_x[0], 16)
            sp.dma_start(x_t[lo, :, :], x_d.rearrange("n c p -> c n p")).then_inc(ld_xt[0], 16)
            sp.dma_start(w_v_s[:, :], w_v).then_inc(ld_w0[0], 16)
            sp.dma_start(w_off_s[:, :, :], w_off).then_inc(ld_w0[1], 16)
            sp.wait_ge(v_ready, 1)
            for i in (1, 0, 3, 4):
                d = (i - WIN) * N
                dst, src = (slice(0, P - d), slice(d, P)) if d > 0 else (slice(-d, P), slice(0, P + d))
                sp.dma_start(v[dst, i, WIN:WIN + W, :], v[src, WIN, WIN:WIN + W, :]).then_inc(v_moved[i], 16)
            sp.dma_start(w_o_s[:, :], w_o).then_inc(ld_w0[3], 16)
            sp.wait_ge(zeroed, 3)
            for b in range(2):
                for half in range(2):
                    cols = slice(b * C + half * CD, b * C + (half + 1) * CD)
                    sp.dma_start(w12_s[half * C:(half + 1) * C, :, cols], w12[b]).then_inc(ld_w12, 16)
            for copy in range(2):
                for half in range(2):
                    rows = slice(copy * C + half * CD, copy * C + (half + 1) * CD)
                    sp.dma_start(wp_s[rows, :, half * C:(half + 1) * C], wp[copy]).then_inc(ld_wp, 16)
            sp.wait_ge(flag_sb, 1)
            count = sp.value_load(vcount[0:1, 0:1], min_val=0, max_val=2 * NC * P)
            with sp.If(count > 0):
                sp.wait_ge(far_row_done, 1)
                pad = (H - 1) * N
                flat = vfar[:, 0:W, :].rearrange("p x c -> p (x c)")
                sp.dma_start(v_dram[0:pad, :], flat[0:pad, :]).then_inc(far_v0, 16)
                sp.dma_start(v_dram[pad + P:, :], flat[0:pad, :]).then_inc(far_v0, 16)
                sp.dma_start(v_dram[pad:pad + P, :],
                             v[:, WIN, WIN:WIN + W, :].rearrange("p x c -> p (x c)")).then_inc(far_v0, 16)
                sp.wait_ge(far_v0, 48)
                with sp.Fori(0, FULL) as k:
                    sp.wait_ge(far_row_done, k + 1)
                    sp.dma_start(vfar[:, PADX:PADX + W, :].rearrange("p x c -> p (x c)"),
                                 v_dram[bass.ds(k * N, P), :]).then_inc(far_v, 16)
            for j, (i0, n) in enumerate(OUT_PARTS):
                sp.wait_ge(res_ready, j + 1)
                sp.dma_start(out_d[i0:i0 + n].rearrange("n c p -> c n p"), res[lo, i0:i0 + n, :]).then_inc(stored, 16)
            sp.wait_ge(stored, 2 * 16 * len(OUT_PARTS))

        @block.gpsimd
        def _(pool):
            nc.gpsimd.memset(ones[:, :], 1.0).then_inc(zeroed, 1)
            nc.gpsimd.memset(g_t[:, :, :, :], 0.0)
            nc.gpsimd.memset(half_pow[:, :], -0.5).then_inc(zeroed, 1)

            def rstd(s, cols):
                pool.wait_ge(var_ready, s + 1)
                nc.gpsimd.tensor_tensor(ab[:, s, 2, 0:cols], ab[:, s, 1, 0:cols], half_pow[:, 0:cols],
                                        ALU.pow).then_inc(rstd_ready, 1)

            pool.wait_ge(zeroed, 2)
            rstd(G0, N)
            nc.gpsimd.memset(w12_s[:, :, :], 0.0)
            nc.gpsimd.memset(wp_s[:, :, :], 0.0)
            nc.gpsimd.memset(wc1_s[:, :], 0.0)
            nc.gpsimd.memset(wc2_s[:, :, :], 0.0).then_inc(zeroed, 1)
            nc.gpsimd.memset(keep[:, :], 1.0).then_inc(zeroed, 1)
            pool.wait_ge(zeroed, 4)
            nc.gpsimd.memset(keep[:, :].rearrange("p (r i) -> p r i", i=W)[:, :, W - 1:W], 0.0)
            nc.gpsimd.memset(g1[:, :, :, :], 0.0)
            nc.gpsimd.memset(pooled[:, :, :, :], 0.0)
            nc.gpsimd.memset(g2[:, :, :, :], 0.0).then_inc(zeroed, 1)
            for s in range(G_IN, NORMS):
                rstd(s, DUO)

        ACT_IMAGES = 6

        @block.scalar
        def _(act):
            act.dma_start(x_b[hi, :, :], x_d[HALF:N].rearrange("n c p -> c n p")).then_inc(ld_x[1], 16)
            act.dma_start(cst[:, :], consts).then_inc(ld_cst, 16)
            act.dma_start(x_t[hi, :, :], x_d.rearrange("n c p -> c n p")).then_inc(ld_xt[1], 16)
            act.dma_start(bias_s[:, :], off_bias.to_broadcast([P, NCH])).then_inc(ld_w0[2], 16)
            act.dma_start(vec_s[:, :], vecs).then_inc(ld_vec, 16)
            act.dma_start(b12_s[:, :], b12).then_inc(ld_vec, 16)
            act.wait_ge(zeroed, 1)
            nc.scalar.activation(warm[:, :], ones[:, :], ACT.Sigmoid)
            act.wait_ge(ld_xt[1], 16)
            act.wait_ge(zeroed, 2)
            act.wait_ge(norm_ready, 1)
            for n in range(ACT_IMAGES):
                nc.scalar.activation(g_t[hi, 0:W, 1:H + 1, n].rearrange("p x y -> p y x"), rows_cols(x_t[hi, n, :]),
                                     ACT.Identity, bias=ab[hi, G0, 3, n:n + 1],
                                     scale=ab[hi, G0, 2, n:n + 1]).then_inc(g_ready, 1)
            act.wait_ge(v_zero, 1)
            act.wait_ge(v_ps, 1)
            for b in range(2):
                last = nc.scalar.activation(v[:, WIN, WIN + b * W // 2:WIN + (b + 1) * W // 2, :],
                                            bank[4 + b][:, :].rearrange("p (x c) -> p x c", c=C), ACT.Copy)
            last.then_inc(v_ready, 1)

            def hats(c):
                x0, w = CHUNKS[c]
                ck = K2 * w * HEADS
                xs = slice(x0, x0 + w)
                act.wait_ge(u_ready, c + 1)
                nc.scalar.activation(mod[:, :, xs, :], u[:, 2 * K2:, xs, :], ACT.Sigmoid).then_inc(mod_ready, 1)
                if c:
                    act.wait_ge(hat_ready, c)
                for d in range(ND):
                    last = nc.scalar.activation(
                        dist[:, d, 0:2 * ck].rearrange("p (k x h) -> p k x h", x=w, h=HEADS),
                        u[:, 0:2 * K2, xs, :], ACT.Abs, bias=float(WIN - d), scale=STEP)
                last.then_inc(dist_done, 1)
                act.wait_ge(dist_done, c + 1)
                if c >= 2:
                    act.wait_ge(hat_used, c - 1)
                nc.scalar.activation(hat[:, c % 2, :, 0:2 * ck], dist[:, :, 0:2 * ck], ACT.Relu, bias=1.0,
                                     scale=-1.0).then_inc(hat_ready, 1)
                act.wait_ge(hat_ready, c + 1)
                nc.scalar.activation(dist[:, WIN, 0:2 * ck], dist[:, WIN, 0:2 * ck], ACT.Relu, bias=-float(WIN),
                                     accum_out=vfar_sum[:, c:c + 1]).then_inc(far_test, 1)
                act.wait_ge(far_test, c + 1)

            def evacuate(c):
                x0, w = CHUNKS[c]
                act.wait_ge(part_used, ND * (c + 1))
                nc.scalar.activation(comb_t[:, x0 // 2:(x0 + w) // 2, :],
                                     comb_bank[:, 0:w * C].rearrange("p (j q) -> p j q", q=P),
                                     ACT.Copy).then_inc(comb_ts, 1)

            hats(0)
            hats(1)
            act.wait_ge(zeroed, 3)
            for half in range(2):
                rows = slice(half * C, (half + 1) * C)
                act.dma_start(wc1_s[rows, rows], wc1).then_inc(ld_c, 16)
                act.dma_start(wc2_s[rows, :, rows], wc2).then_inc(ld_c, 16)
            for c in range(NC):
                evacuate(c)
                if c + 2 < NC:
                    hats(c + 2)

            act.wait_ge(zeroed, 5)
            for g in range(2):
                act.wait_ge(norm_ready, G_IN + g + 1)
                for j in range(DUO):
                    n = DUO * g + j
                    nc.scalar.activation(inner(g1, n, 1)[:, 0], rows_cols(x1[:, n, :]), ACT.Identity,
                                         bias=ab[:, G_IN + g, 3, j:j + 1],
                                         scale=ab[:, G_IN + g, 2, j:j + 1]).then_inc(g1_ready, 1)
            act.wait_ge(ld_vec, 32)
            for g in range(2):
                act.wait_ge(r12_ps, g + 1)
                if g:
                    act.wait_ge(r12_used, 1)
                nc.scalar.activation(r12[:, 0].rearrange("p n (x y) -> p n y x", y=H),
                                     bank[g][lo, :].rearrange("p (n y x) -> p n y x", n=DUO, x=W), ACT.Relu,
                                     bias=b12_s[lo, 0:1])
                nc.scalar.activation(r12[:, 1], bank[g][hi, :].rearrange("p (n q) -> p n q", n=DUO), ACT.Relu,
                                     bias=b12_s[hi, 0:1]).then_inc(r12_ready, 1)
            for g in range(2):
                act.wait_ge(norm_ready, G_C1 + g + 1)
                for j in range(DUO):
                    last = nc.scalar.activation(c_aff[:, DUO * g + j, :], bank[2 + g][:, j * HW:(j + 1) * HW],
                                                ACT.Identity, bias=ab[:, G_C1 + g, 3, j:j + 1],
                                                scale=ab[:, G_C1 + g, 2, j:j + 1])
                last.then_inc(caff_ready, 1)
            for n in range(HALF):
                g, j = n // DUO, n % DUO
                act.wait_ge(pre_ready, n + 1)
                nc.scalar.activation(inner(g2, n, 1)[:, 0], rows_cols(pre[:, n, :]), ACT.Relu,
                                     bias=ab[:, G_P + g, 3, j:j + 1]).then_inc(g2_ready, 1)
            for k, (i0, n) in enumerate(OUT_PARTS):
                act.wait_ge(o_ps, k + 1)
                nc.scalar.activation(res[:, i0:i0 + n, :], out_banks[k][:, 0:n * HW].rearrange("p (n q) -> p n q", n=n),
                                     ACT.Relu, bias=vec_s[:, 4:5]).then_inc(relu_ready, 1)
            for k, (i0, n) in enumerate(OUT_PARTS):
                act.wait_ge(res_ready, k + 1)
                act.dma_start(out_d[HALF + i0:HALF + i0 + n].rearrange("n c p -> c n p"),
                              res[hi, i0:i0 + n, :]).then_inc(stored, 16)

        @block.vector
        def _(ve):
            steps = [0]

            def tick(ins):
                steps[0] += 1
                ins.then_inc(step, 1)
                return steps[0]

            def link(ins):
                ve.wait_ge(step, tick(ins))

            def norm_stats(s, views):
                cols = len(views)
                for n, view in enumerate(views):
                    last = nc.vector.bn_stats(bn[:, s, n, :], view)
                link(last)
                for n in range(cols):
                    last = nc.vector.bn_aggr(mv[:, s, n, :], bn[:, s, n, :])
                link(last)
                link(nc.vector.tensor_tensor(sq[:, s, 0:cols], mv[:, s, 0:cols, 0], mv[:, s, 0:cols, 0], ALU.mult))
                nc.vector.tensor_tensor(mv[:, s, 0:cols, 1], mv[:, s, 0:cols, 1], sq[:, s, 0:cols],
                                        ALU.add).then_inc(stats_in, 1)

            def variance(s, cols, stat):
                ve.wait_ge(stats_ps, s + 1)
                link(nc.vector.tensor_copy(ab[:, s, 0:2, 0:cols], stat.rearrange("p (n t) -> p t n", t=2)))
                link(nc.vector.tensor_tensor(sq[:, s, 0:cols], ab[:, s, 0, 0:cols], ab[:, s, 0, 0:cols], ALU.mult))
                nc.vector.scalar_tensor_tensor(ab[:, s, 1, 0:cols], ab[:, s, 1, 0:cols], EPS, sq[:, s, 0:cols],
                                               ALU.add, ALU.subtract).then_inc(var_ready, 1)

            def affine(s, cols, gamma=None, beta=None, extra=None):
                ve.wait_ge(rstd_ready, s + 1)
                scale, shift = ab[:, s, 2, 0:cols], ab[:, s, 3, 0:cols]
                if gamma is not None:
                    link(nc.vector.tensor_scalar(scale, scale, gamma, None, ALU.mult))
                ins = nc.vector.scalar_tensor_tensor(shift, ab[:, s, 0, 0:cols], -1.0, scale, ALU.mult, ALU.mult)
                if beta is not None:
                    link(ins)
                    ins = nc.vector.tensor_scalar(shift, shift, beta, extra, ALU.add, ALU.add)
                ins.then_inc(norm_ready, 1)

            def far_displacements():
                def wait(n):
                    ve.wait_ge(far, n)

                def run(base, steps):
                    for j, ins in enumerate(steps):
                        ins().then_inc(far, 1)
                        wait(base + j + 1)
                    ve.sem_inc(far_runs, 1)
                    return base + len(steps)

                ux = u[:, 0:K2, :, :].rearrange("p k x h -> p k (x h)")
                uy = u[:, K2:2 * K2, :, :].rearrange("p k x h -> p k (x h)")
                m = mod[:, :, :, :].rearrange("p k x h -> p k (x h)")
                middle = vfar[:, PADX:PADX + W, :]

                def hat_steps(a, src, i):
                    t = fdist[:, a]
                    ramp = cst[:, bass.ds(C_RAMP + i, 1)]
                    return [lambda: nc.vector.tensor_copy(fmove[:, :], ramp),
                            lambda: nc.vector.tensor_scalar(t, src, STEP, fmove[:, 0:1], ALU.mult, ALU.subtract),
                            lambda: nc.vector.scalar_tensor_tensor(t, t, -1.0, t, ALU.mult, ALU.min),
                            lambda: nc.vector.tensor_scalar(t, t, 1.0, 0.0, ALU.add, ALU.max)]

                def row_steps(i):
                    return hat_steps(1, uy, i) + [
                        lambda: nc.vector.tensor_tensor(fdist[:, 1], fdist[:, 1], m, ALU.mult)]

                def cell_steps(i):
                    return hat_steps(0, ux, i) + [
                        lambda: nc.vector.tensor_tensor(fprod, fdist[:, 0], fdist[:, 1], ALU.mult),
                        lambda: nc.vector.tensor_reduce(fcell[:, :], fprod.rearrange("p k q -> p q k"),
                                                        AX_X, ALU.add),
                        lambda: nc.vector.tensor_tensor(
                            fpart.rearrange("p x (h e) -> p (x h) e", e=HD),
                            vfar[:, bass.ds(i, W), :].rearrange("p x (h e) -> p (x h) e", e=HD),
                            fcell[:, :].unsqueeze(2).to_broadcast([P, W * HEADS, HD]), ALU.mult),
                        lambda: nc.vector.tensor_tensor(far_sum, far_sum, fpart, ALU.add)]

                CELL = 8

                def columns(base, i0, i1):
                    with ve.Fori(i0, i1) as i:
                        run(base + (i - i0) * CELL, cell_steps(i))
                    return base + (i1 - i0) * CELL

                ve.wait_ge(part_used, ND * NC)
                n = run(0, [lambda: nc.vector.memset(vfar[:, :, :], 0.0),
                            lambda: nc.vector.memset(far_sum, 0.0)])
                ve.sem_inc(far_row_done, 1)
                for r0, r1, ranges in FAR_ROWS:
                    per_row = 5 + sum(i1 - i0 for i0, i1 in ranges) * CELL
                    with ve.Fori(r0, r1) as k:
                        base = n + (k - r0) * per_row
                        ve.wait_ge(far_v, (k + 1) * 16)
                        base = run(base, row_steps(k))
                        for i0, i1 in ranges:
                            base = columns(base, i0, i1)
                        ve.sem_inc(far_row_done, 1)
                    n += per_row * (r1 - r0)
                ve.sem_inc(far_ts, 1)
                ve.wait_ge(far_tp, 1)
                for b in range(2):
                    last = nc.vector.tensor_copy(far_t[:, b * W // 4:(b + 1) * W // 4, :],
                                                 bank[b][:, :].rearrange("p (j q) -> p j q", q=P))
                last.then_inc(far_ts, 1)
                ve.wait_ge(far_y, 1)
                for par in range(2):
                    t = x_b[:, :, :].rearrange("p n (y j a) -> p a j y n", a=2, j=W // 2)[:, par]
                    nc.vector.tensor_tensor(t, bank[2 + par][:, :].rearrange("p (j y n) -> p j y n", y=H, n=HALF), t,
                                            ALU.add).then_inc(far_added, 1)
                ve.wait_ge(far_added, 2)

            nc.vector.memset(v[:, :, :, :], 0.0).then_inc(v_zero, 1)
            for half in range(2):
                ve.wait_ge(ld_x[half], 16)
            norm_stats(G0, [x_b[:, n, :] for n in range(HALF)])
            variance(G0, N, bank[7][:, 0:2 * N])
            affine(G0, N)
            ve.wait_ge(norm_ready, 1)
            ve.wait_ge(ld_xt[0], 16)
            ve.wait_ge(zeroed, 2)
            for n in range(N):
                nc.vector.tensor_scalar(g_t[lo, 1:W + 1, 1:H + 1, n].rearrange("p x y -> p y x"),
                                        rows_cols(x_t[lo, n, :]), ab[lo, G0, 2, n:n + 1], ab[lo, G0, 3, n:n + 1],
                                        ALU.mult, ALU.add).then_inc(g_ready, 1)
            ve.wait_ge(ld_xt[1], 16)
            for n in range(ACT_IMAGES, N):
                nc.vector.tensor_scalar(g_t[hi, 0:W, 1:H + 1, n].rearrange("p x y -> p y x"),
                                        rows_cols(x_t[hi, n, :]), ab[hi, G0, 2, n:n + 1], ab[hi, G0, 3, n:n + 1],
                                        ALU.mult, ALU.add).then_inc(g_ready, 1)
            ve.wait_ge(ld_w0[2], 16)

            def offsets(c):
                x0, w = CHUNKS[c]
                ve.wait_ge(off_ps, c + 1)
                for b in range(w // 2):
                    xa = x0 + 2 * b
                    last = nc.vector.tensor_tensor(
                        u[:, :, xa:xa + 2, :].rearrange("p k x h -> p x k h"),
                        bank[2 * (c % 2) + b][:, 0:2 * NCH].rearrange("p (x k h) -> p x k h", x=2, h=HEADS),
                        bias_s[:, :].rearrange("p (k h) -> p k h", h=HEADS).unsqueeze(1).to_broadcast(
                            [P, 2, 3 * K2, HEADS]), ALU.add)
                last.then_inc(u_ready, 1)

            applied = [0]

            def chunk(c):
                x0, w = CHUNKS[c]
                cx = w * HEADS
                ck = K2 * cx
                cv = w * C
                made = {}

                def product(i):
                    nd, d0 = 2 * DX[i] + 1, WIN - DX[i]
                    return nc.vector.tensor_tensor(prod[:, PROD_SLOT[i], 0:nd, 0:ck], hat[:, c % 2, d0:d0 + nd, 0:ck],
                                                   wy[:, i:i + 1, 0:ck].to_broadcast([P, nd, ck]), ALU.mult)

                def tap_sum(i, slot):
                    nd = 2 * DX[i] + 1
                    ve.wait_ge(step, made["product", i])
                    made["sum", i] = tick(nc.vector.tensor_reduce(
                        cell[:, slot, 0:nd, 0:cx],
                        prod[:, PROD_SLOT[i], 0:nd, 0:ck].rearrange("p d (k q) -> p d q k", k=K2), AX_X, ALU.add))

                def apply(i, slot=None):
                    nd = 2 * DX[i] + 1
                    n = applied[0]
                    applied[0] += 1
                    if c == 0:
                        if i == WIN:
                            ve.wait_ge(v_ready, 1)
                        else:
                            ve.wait_ge(v_moved[i], 16)
                    if n >= PARTS:
                        ve.wait_ge(part_used, n - PARTS + 1)
                    if i in PE_ROWS:
                        k = PE_ROWS.index(i)
                        ve.wait_ge(cell_ps, len(PE_ROWS) * (c + 1))
                        weights = cell_bank[:, k * ND * CXM:k * ND * CXM + nd * cx].rearrange("p (d q) -> p d q", d=nd)
                    else:
                        ve.wait_ge(step, made["sum", i])
                        weights = cell[:, slot, 0:nd, 0:cx]
                    xa = x0 + WIN - DX[i]
                    v0 = v[:, i, xa:xa + w, :]
                    moved = bass.AP(v0.tensor, v0.offset, [v0.ap[0], [C, nd], [HD, cx], [1, HD]])
                    nc.vector.tensor_tensor(part[:, n % PARTS, 0:nd, 0:cv].rearrange("p d (q e) -> p d q e", e=HD),
                                            moved, weights.unsqueeze(3).to_broadcast([P, nd, cx, HD]),
                                            ALU.mult).then_inc(part_ready, 1)

                ve.wait_ge(hat_ready, c + 1)
                ve.wait_ge(mod_ready, c + 1)
                if c:
                    ve.wait_ge(step, last_made[0])
                made_wy = tick(nc.vector.tensor_tensor(
                    wy[:, :, 0:ck].rearrange("p d (k q) -> p d k q", k=K2),
                    hat[:, c % 2, :, ck:2 * ck].rearrange("p d (k q) -> p d k q", k=K2),
                    mod[:, :, x0:x0 + w, :].rearrange("p k x h -> p k (x h)").unsqueeze(1).to_broadcast(
                        [P, ND, K2, cx]), ALU.mult))
                nc.vector.tensor_tensor_reduce(out=edge[:, 0:ck], in0=hat[:, c % 2, WIN, 0:ck],
                                               in1=hat[:, c % 2, WIN, ck:2 * ck], scale=1.0, scalar=2.0,
                                               op0=ALU.add, op1=ALU.min, accum_out=vmin[:, c:c + 1])
                ve.wait_ge(step, made_wy)
                for k, i in enumerate(PE_ROWS):
                    product(i).then_inc(prod_ready, 1)
                made["product", 2] = tick(product(2))
                tap_sum(2, 0)
                made["product", 0] = tick(product(0))
                apply(2, 0)
                if c == NC - 1:
                    window_test()
                apply(1)
                tap_sum(0, 1)
                product(4).then_inc(hat_used, 1)
                apply(0, 1)
                if c == NC - 1:
                    ve.wait_ge(flag_ps, 1)
                    link(nc.vector.tensor_reduce(vtotal[:, :], bank[1][0:1, 0:2 * NC], AX_X, ALU.add))
                    nc.vector.tensor_copy(vcount[:, :], vtotal[:, :]).then_inc(flag_sb, 1)
                ve.wait_ge(hat_used, c + 1)
                made["product", 4] = 0
                tap_sum(4, 0)
                apply(3)
                apply(4, 0)

            def window_test():
                ve.wait_ge(far_test, NC)
                nc.vector.tensor_scalar(vflag[:, 0, :], vmin[:, :], 0.0, None, ALU.is_le)
                nc.vector.tensor_scalar(vflag[:, 1, :], vfar_sum[:, :], 0.0, None, ALU.is_gt).then_inc(flag_in, 1)

            last_made = [0]
            offsets(0)
            for c in range(NC):
                if c + 1 < NC:
                    offsets(c + 1)
                chunk(c)
                last_made[0] = steps[0]
            count = ve.value_load(vcount[0:1, 0:1], min_val=0, max_val=2 * NC * P)
            with ve.If(count > 0):
                far_displacements()

            ve.wait_ge(y0_ps, NC)
            for par in range(2):
                def column_pairs(t):
                    return t[:, :, :].rearrange("p n (y j a) -> p a j y n", a=2, j=W // 2)[:, par]
                last = nc.vector.tensor_tensor(
                    column_pairs(x1), y0_banks[par][:, :].rearrange("p (j y n) -> p j y n", y=H, n=HALF),
                    column_pairs(x_b), ALU.add)
            link(last)
            for g in range(2):
                norm_stats(G_IN + g, [x1[:, DUO * g + j, :] for j in range(DUO)])
            for g in range(2):
                variance(G_IN + g, DUO, pair_stats(G_IN + g))
            for g in range(2):
                affine(G_IN + g, DUO)

            ve.wait_ge(ld_vec, 32)
            for g in range(2):
                ve.wait_ge(c_ps, g + 1)
                norm_stats(G_C1 + g, [bank[2 + g][:, j * HW:(j + 1) * HW] for j in range(DUO)])

            def reverse(ap):
                n = ap.ap[-1][1]
                return bass.AP(ap.tensor, ap.offset + n - 1, [ap.ap[0], [-1, n]])

            def pool_pair(g):
                ve.wait_ge(r12_ready, g + 1)
                flat_in = r12.rearrange("p b n q -> p (b n q)")
                flat_out = maxima.rearrange("p b n q -> p (b n q)")
                ins = nc.vector.tensor_tensor_scan(reverse(flat_out), reverse(keep[:, :]), reverse(flat_in), 0.0,
                                                   ALU.mult, ALU.max)
                ins.then_inc(r12_used, 1)
                ve.wait_ge(r12_used, g + 1)
                top = maxima[:, 0].rearrange("p n (x y) -> p n y x", y=H)
                left = maxima[:, 1].rearrange("p n (y x) -> p n y x", x=W)
                n0 = DUO * g
                nc.vector.tensor_tensor(inner(pooled, n0, DUO, lo), top, left, ALU.add)
                nc.vector.tensor_tensor(pooled[hi, n0:n0 + DUO, 1:H + 1, 0:W], top, left,
                                        ALU.add).then_inc(pooled_ready, 1)

            ve.wait_ge(zeroed, 5)
            pool_pair(0)
            for g in range(2):
                variance(G_C1 + g, DUO, pair_stats(G_C1 + g))
            for g in range(2):
                affine(G_C1 + g, DUO, vec_s[:, 2:3], vec_s[:, 3:4], vec_s[:, 1:2])
            pool_pair(1)

            for g in range(2):
                ve.wait_ge(p_ps, g + 1)
                norm_stats(G_P + g, [bank[4 + g][:, j * HW:(j + 1) * HW] for j in range(DUO)])
                variance(G_P + g, DUO, pair_stats(G_P + g))
                affine(G_P + g, DUO, vec_s[:, 0:1])
                ve.wait_ge(norm_ready, G_P + g + 1)
                ve.wait_ge(caff_ready, g + 1)
                for j in range(DUO):
                    nc.vector.scalar_tensor_tensor(pre[:, DUO * g + j, :], bank[4 + g][:, j * HW:(j + 1) * HW],
                                                   ab[:, G_P + g, 2, j:j + 1], c_aff[:, DUO * g + j, :], ALU.mult,
                                                   ALU.add).then_inc(pre_ready, 1)
            for k, (i0, n) in enumerate(OUT_PARTS):
                ve.wait_ge(relu_ready, k + 1)
                nc.vector.tensor_tensor(res[:, i0:i0 + n, :], res[:, i0:i0 + n, :], x1[:, i0:i0 + n, :],
                                        ALU.add).then_inc(res_ready, 1)

        @block.tensor
        def _(pe):
            ident = cst[:, C_ID:C_ID + P]

            def group_means(s, cols, out_ap, mats):
                pe.wait_ge(stats_in, s + 1)
                for i, m in enumerate(mats):
                    last = nc.tensor.matmul(out_ap[:, 2 * cols * i:2 * cols * (i + 1)], cst[:, m:m + P],
                                            mv[:, s, 0:cols, :].rearrange("p n t -> p (n t)"), start=True, stop=True)
                last.then_inc(stats_ps, 1)

            pe.wait_ge(ld_cst, 16)
            group_means(G0, HALF, bank[7], (C_GT, C_GT + P))

            pe.wait_ge(g_ready, 2 * N)
            pe.wait_ge(ld_w0[0], 16)
            for j in range(W // 2):
                last = nc.tensor.matmul(bank[4 + j // 4][:, (j % 4) * P:(j % 4 + 1) * P],
                                        g_t[:, 2 * j + 1, 1:H + 1, :].rearrange("p y n -> p (y n)"), w_v_s[:, :],
                                        start=True, stop=True)
            last.then_inc(v_ps, 1)

            def conv_column(c, j):
                x0, w = CHUNKS[c]
                if c >= 2 and j == 0:
                    pe.wait_ge(u_ready, c - 1)
                for t in range(2 * KS):
                    ky, single = t // 2, t % 2
                    last = nc.tensor.matmul(
                        bank[2 * (c % 2) + j // 2][:, (j % 2) * NCH:(j % 2 + 1) * NCH],
                        g_t[:, x0 + j + 2 * single, ky:ky + H, :].rearrange("p y n -> p (y n)"), w_off_s[:, t, :],
                        start=(t == 0), stop=(t == 2 * KS - 1))
                if j == w - 1:
                    last.then_inc(off_ps, 1)

            def tap_sum(c, k):
                i, w = PE_ROWS[k], CHUNKS[c][1]
                nd, cx = 2 * DX[i] + 1, w * HEADS
                pe.wait_ge(prod_ready, len(PE_ROWS) * c + k + 1)
                for t in range(K2):
                    last = nc.tensor.matmul(
                        cell_bank[:, k * ND * CXM:k * ND * CXM + nd * cx].rearrange("p (d q) -> p d q", d=nd), ident,
                        prod[:, PROD_SLOT[i], 0:nd, t * cx:(t + 1) * cx], start=(t == 0), stop=(t == K2 - 1))
                last.then_inc(cell_ps, 1)

            def row_sum(c, m):
                w, i = CHUNKS[c][1], APPLY[m]
                n = ND * c + m
                nd = 2 * DX[i] + 1
                pe.wait_ge(part_ready, n + 1)
                for d in range(nd):
                    for j in range(w // 2):
                        last = nc.tensor.matmul(comb_bank[:, j * P:(j + 1) * P], part[:, n % PARTS, d, j * P:(j + 1) * P], ident,
                                                start=(m == 0 and d == 0 and j == 0),
                                                stop=(m == ND - 1 and d == nd - 1 and j == w // 2 - 1),
                                                is_transpose=True)
                last.then_inc(part_used, 1)

            def project(out_banks, src, j0, j1, done):
                for par in range(2):
                    rows = slice(par * C, (par + 1) * C)
                    for half in range(2):
                        last = nc.tensor.matmul(
                            out_banks[par][half * C:(half + 1) * C, j0 * C:j1 * C], w_o_s[rows, :],
                            src[rows, j0:j1, :].rearrange("p j (y n) -> p j y n", n=N)[
                                :, :, :, half * HALF:(half + 1) * HALF], start=True, stop=True)
                last.then_inc(done, 1)

            def y0(c):
                x0, w = CHUNKS[c]
                pe.wait_ge(comb_ts, c + 1)
                project(y0_banks, comb_t, x0 // 2, (x0 + w) // 2, y0_ps)

            pe.wait_ge(ld_w0[1], 16)
            for c in range(2):
                if c == 1:
                    pe.wait_ge(v_ready, 1)
                    pe.wait_ge(ld_w0[3], 16)
                for j in range(CHUNKS[c][1]):
                    conv_column(c, j)
            for c in range(NC):
                for k in range(len(PE_ROWS)):
                    tap_sum(c, k)
                if c:
                    y0(c - 1)
                if c == NC - 1:
                    pe.wait_ge(flag_in, 1)
                    nc.tensor.matmul(bank[1][0:1, 0:2 * NC], ones[:, :],
                                     vflag[:, :, :].rearrange("p a c -> p (a c)"), start=True,
                                     stop=True).then_inc(flag_ps, 1)
                columns = CHUNKS[c + 2][1] if c + 2 < NC else 0
                for m in range(ND):
                    if m < columns:
                        conv_column(c + 2, m)
                    if c == NC - 1 and m == ND - 1:
                        pe.wait_ge(flag_sb, 1)
                        count = pe.value_load(vcount[0:1, 0:1], min_val=0, max_val=2 * NC * P)
                    row_sum(c, m)
            y0(NC - 1)
            with pe.If(count > 0):
                pe.wait_ge(far_ts, 1)
                for j in range(W // 2):
                    last = nc.tensor.transpose(bank[j // 4][:, (j % 4) * P:(j % 4 + 1) * P],
                                               far_sum[:, 2 * j:2 * j + 2, :].rearrange("p x c -> p (x c)"), ident)
                last.then_inc(far_tp, 1)
                pe.wait_ge(far_ts, 2)
                project(bank[2:4], far_t, 0, W // 2, far_y)

            for g in range(2):
                group_means(G_IN + g, DUO, pair_stats(G_IN + g), (C_GB,))
            pe.wait_ge(ld_w12, 64)
            pe.wait_ge(ld_c, 64)

            def images(ap, n=DUO):
                return ap.rearrange("p (n y x) -> p n y x", n=n, x=W)

            for g in range(2):
                n0 = DUO * g
                pe.wait_ge(g1_ready, n0 + DUO)
                nc.tensor.matmul(images(bank[2 + g][:, :]), wc1_s[:, :], inner(g1, n0, DUO), start=True,
                                 stop=True).then_inc(c_ps, 1)
                for t in range(K2):
                    ky, kx = t // KS, t % KS
                    last = nc.tensor.matmul(images(bank[g][:, :]), w12_s[:, t, :],
                                            g1[:, n0:n0 + DUO, ky:ky + H, kx:kx + W],
                                            start=(t == 0), stop=(t == K2 - 1))
                last.then_inc(r12_ps, 1)
            for g in range(2):
                group_means(G_C1 + g, DUO, pair_stats(G_C1 + g), (C_GB,))
            pe.wait_ge(ld_wp, 64)
            for g in range(2):
                n0 = DUO * g
                pe.wait_ge(pooled_ready, g + 1)
                for t in range(2 * KS):
                    ky, kx = t // 2, 2 * (t % 2)
                    last = nc.tensor.matmul(images(bank[4 + g][:, :]), wp_s[:, t, :],
                                            pooled[:, n0:n0 + DUO, ky:ky + H, kx:kx + W],
                                            start=(t == 0), stop=(t == 2 * KS - 1))
                    if g == 1 and t == KS:
                        group_means(G_P, DUO, pair_stats(G_P), (C_GB,))
                last.then_inc(p_ps, 1)
            for k, (i0, n) in enumerate(OUT_PARTS):
                pe.wait_ge(g2_ready, i0 + n)
                for t in range(K2):
                    ky, kx = t // KS, t % KS
                    last = nc.tensor.matmul(images(out_banks[k][:, 0:n * HW], n), wc2_s[:, t, :],
                                            g2[:, i0:i0 + n, ky:ky + H, kx:kx + W],
                                            start=(t == 0), stop=(t == K2 - 1))
                    if k == 0 and t == KS:
                        group_means(G_P + 1, DUO, pair_stats(G_P + 1), (C_GB,))
                last.then_inc(o_ps, 1)


_LAYOUT = ("x", "consts", "w_off", "w_v", "off_bias", "w_o", "w12", "b12", "wp", "wc1", "wc2", "vecs")


def kernel(**inputs):
    import numpy as _np
    import concourse.bacc as _bacc
    from concourse import mybir as _mybir
    from concourse.bass_utils import run_bass_kernel_spmd as _run

    a = {k: _np.asarray(v) for k, v in inputs.items()}
    l0 = {k[8:]: v for k, v in a.items() if k.startswith("L0_conv_")}
    l1 = {k[8:]: v for k, v in a.items() if k.startswith("L1_conv_")}
    z = _np.zeros

    def by_tap(off, attn):
        off = off.reshape((HEADS, K2, 2) + off.shape[1:])
        attn = attn.reshape((1, HEADS, K2) + attn.shape[1:])
        both = _np.concatenate([_np.moveaxis(off, 2, 0), attn])
        return _np.swapaxes(both, 1, 2).reshape((NCH,) + attn.shape[3:])

    w = by_tap(l0["off_w"], l0["attn_w"]).transpose(1, 2, 3, 0)
    w_off = z((P, 2 * KS, NCH), _np.float32)
    w_off[:C, 0::2] = w[:, :, 0]
    w_off[C:, 0::2] = w[:, :, 1]
    w_off[:C, 1::2] = w[:, :, 2]
    w_v = z((P, P), _np.float32)
    w_v[:C, :C] = w_v[C:, C:] = l0["Wv"].T
    taps = lambda t: t.transpose(1, 2, 3, 0).reshape(t.shape[1], K2, t.shape[0])
    wp = taps(l1["p_w"]).reshape(CD, KS, KS, C)
    wp_pair = z((2, CD, 2 * KS, C), _np.float32)
    wp_pair[0, :, 0::2], wp_pair[1, :, 0::2], wp_pair[0, :, 1::2] = wp[:, :, 0], wp[:, :, 1], wp[:, :, 2]
    twice = lambda t: _np.concatenate([t, t])
    arrays = {
        "x": a["x"], "consts": shape_constants(), "w_off": w_off, "w_v": w_v,
        "off_bias": by_tap(l0["off_b"], l0["attn_b"]).reshape(1, NCH),
        "w_o": twice(l0["Wo"].T),
        "w12": _np.stack([taps(l1["p1_w"]), taps(l1["p2_w"])]),
        "b12": _np.concatenate([twice(l1["p1_b"]), twice(l1["p2_b"])]).reshape(P, 1),
        "wp": wp_pair, "wc1": l1["c1_w"][:, :, 0, 0].T, "wc2": taps(l1["c2_w"]),
        "vecs": _np.stack([twice(l1[k]) for k in ("p_gn_g", "p_gn_b", "gn1_g", "gn1_b", "c2_b")], 1),
    }
    nc = _bacc.Bacc("TRN2", target_bir_lowering=False, num_devices=1)
    feed, args = {}, []
    for name in _LAYOUT:
        t = _np.ascontiguousarray(arrays[name])
        feed[f"in_{name}"] = t
        args.append(nc.dram_tensor(f"in_{name}", t.shape, _mybir.dt.from_np(t.dtype), kind="ExternalInput").ap())
    args.append(nc.dram_tensor("out_0", (N, C, H, W), F32, kind="ExternalOutput").ap())
    build(nc, *args)
    return _run(nc, [feed], core_ids=[0]).results[0]["out_0"]
```

```python
from contextlib import ExitStack

import numpy as np

import concourse.bass as bass
from concourse import mybir

ALU = mybir.AluOpType
ACT = mybir.ActivationFunctionType
F32 = mybir.dt.float32
F32R = mybir.dt.float32r
I32 = mybir.dt.int32
AX_X = mybir.AxisListType.X

N, C, H, W = 8, 64, 16, 16
HEADS, KS = 8, 3
K2 = KS * KS
HD = C // HEADS
CD = 32
P = 128
HALF = N // 2
DUO = 2
HW = H * W
PW = W + 2
NCH = 3 * K2 * HEADS
KHW = K2 * HEADS * W
EPS = 1e-5
LO_ROW = 32
STEP = 0.5 * (W - 1) * (2.0 / W)
CHUNKS = ((0, 2), (2, 4), (6, 4), (10, 4), (14, 2))
NC = len(CHUNKS)
XM = 4
CKM = K2 * XM * HEADS
CXM = XM * HEADS
CVM = XM * C
CONV_BANKS = ((1,), (0, 1), (0, 1), (0, 1), (0,))
WIN = 2
ND = 2 * WIN + 1
PADX = W - 1
VW = W + 2 * PADX
FULL = 2 * (W - 1) + 1
DX = [1, 2, 2, 2, 1]
ROWS = (2, 1, 3, 0, 4)
CELL0 = {2: 0, 1: 5, 3: 10, 0: 15, 4: 18}
CELLS = 21
GROUPS = ((0, 8, 2), (8, 15, 3), (15, 18, 4))
OWN_ROW = 4
APPLY = (4, 2, 1, 3, 0)
RANGES = ((0, 5), (5, 9), (9, PW))
BEFORE = (0, 1, 2, 0, 0)
BETWEEN = (3, 2, 2, 0, 0)
WARM_START, WARM_CHUNK = 20, (0, 0, 0, 16, 10)
WARM_IN = (11, 14)
WARM_P = 12
PARTS = 3

FAR_ROWS = [(0, PADX - WIN, [(0, FULL)]),
            (PADX - WIN, PADX - WIN + 1, [(0, PADX - 1), (PADX + 2, FULL)]),
            (PADX - WIN + 1, PADX + WIN, [(0, PADX - WIN), (PADX + WIN + 1, FULL)]),
            (PADX + WIN, PADX + WIN + 1, [(0, PADX - 1), (PADX + 2, FULL)]),
            (PADX + WIN + 1, FULL, [(0, FULL)])]

G0, G_IN, G_C1, G_P, NORMS = 0, 1, 3, 4, 7

C_GB = 0
C_GT = C_GB + P
C_RAMP = C_GT + 2 * P
C_ID = C_RAMP + 2 * W - 1
NCONST = C_ID + P


def shape_constants():
    c = np.zeros((P, NCONST), np.float32)
    i = np.arange(P)
    c[i, C_ID + i] = 1
    same_group = (i[:, None] % C) // 2 == (i[None, :] % C) // 2
    c[:, C_GB:C_GB + P] = 0.5 * (same_group & (i[:, None] // C == i[None, :] // C))
    for half in range(2):
        c[:, C_GT + half * P:C_GT + (half + 1) * P] = 0.5 * (same_group & (i[:, None] // C == half))
    c[:, C_RAMP:C_RAMP + 2 * W - 1] = np.arange(1 - W, W)
    return c


def build(nc, x, consts, w_off, w_v, off_bias, w_o, w12, b12, wp, wc1, wc2, vecs, out):
    with ExitStack() as ctx:
        def sb(name, shape, dt=F32):
            return ctx.enter_context(nc.sbuf_tensor(name, shape, dt))

        def sem(name):
            return ctx.enter_context(nc.semaphore(name))

        cst = sb("cst", [P, NCONST])
        x_b = sb("x_b", [P, HALF, HW])
        staging = sb("staging", [P, 2 * K2 * P])
        x_t = staging[0:C, 0:N * HW].rearrange("p (n q) -> p n q", n=N)
        raw = staging[:, :].rearrange("p (b t q) -> p b t q", b=2, q=P)
        raw_c1 = sb("raw_c1", [P, P])
        w_v_s = sb("w_v_s", [P, C])
        bias_s = sb("bias_s", [P, NCH])
        bias_r = sb("bias_r", [P, NCH], F32R)
        ones_r = sb("ones_r", [P, P], F32R)
        u = sb("u", [P, 3 * K2, W, HEADS])
        mod = sb("mod", [P, K2, W, HEADS])
        beyond = sb("beyond", [P, 2 * CKM])
        hat = sb("hat", [P, 2, ND, 2 * CKM])
        wy = sb("wy", [P, ND, CKM])
        prod = sb("prod", [P, CELLS * CKM])
        cell_t = sb("cell_t", [P, 5, P])
        cell = sb("cell", [P, 3, CXM])
        v = sb("v", [P, ND, W + 2 * WIN, C])
        part = sb("part", [P, PARTS, ND, CVM])
        comb_t = sb("comb_t", [P, W // 2, P])
        w_o_s = sb("w_o_s", [P, C])
        edge = sb("edge", [P, CKM])
        vmin = sb("vmin", [P, NC])
        vfar_sum = sb("vfar_sum", [P, NC])
        vflag = sb("vflag", [P, 2, NC])
        vtotal = sb("vtotal", [1, 1])
        vcount = sb("vcount", [1, 1], I32)
        ones = sb("ones", [P, 1])
        warm = sb("warm", [P, 1])
        vfar = part[:, :, :, :].rearrange("p b d s -> p (b d s)")[:, 0:VW * C].rearrange("p (x c) -> p x c", c=C)
        fmove = sb("fmove", [P, 1])
        fcell = sb("fcell", [P, W * HEADS])
        hat_flat = hat[:, :, :, :].rearrange("p b d s -> p (b d s)")
        fdist = hat_flat[:, 0:2 * KHW].rearrange("p (a k q) -> p a k q", a=2, k=K2)
        fprod = hat_flat[:, 2 * KHW:3 * KHW].rearrange("p (k q) -> p k q", k=K2)
        fpart = hat_flat[:, 3 * KHW:3 * KHW + W * C].rearrange("p (x c) -> p x c", c=C)
        far_sum = prod[:, 0:W * C].rearrange("p (x c) -> p x c", c=C)
        far_t = prod[:, W * C:2 * W * C].rearrange("p (j q) -> p j q", q=P)
        vec_s = sb("vec_s", [P, 5])
        b12_s = sb("b12_s", [P, 1])
        bn = sb("bn", [P, NORMS, HALF, 6])
        mv = sb("mv", [P, NORMS, HALF, 2])
        sq = sb("sq", [P, NORMS, N])
        ab = sb("ab", [P, NORMS, 4, N])
        half_pow = sb("half_pow", [P, N])
        w_raw = prod[:, 0:K2 * NCH].rearrange("p (t q) -> p t q", q=NCH)
        with ExitStack() as conv_scope:
            def conv_sb(name, shape, dt=F32R):
                return conv_scope.enter_context(nc.sbuf_tensor(name, shape, dt))

            g_t = conv_sb("g_t", [C, PW, PW, N], F32)
            g_pair = conv_sb("g_pair", [P, PW, PW, N])
            g_cross = conv_sb("g_cross", [P, PW, PW, N])
            w_pair = conv_sb("w_pair", [P, 2 * KS, NCH])
            w_v_pair = conv_sb("w_v_pair", [P, C])
            w_v_cross = conv_sb("w_v_cross", [P, C])
            w_cross = conv_sb("w_cross", [P, K2, NCH])
        x1 = sb("x1", [P, HALF, HW])
        g1_h, g1_l = (sb(f"g1_{k}", [P, HALF, PW, PW], F32R) for k in "hl")
        w12_h, w12_l = (sb(f"w12_{k}", [P, K2, P], F32R) for k in "hl")
        wc1_h, wc1_l = (sb(f"wc1_{k}", [P, P], F32R) for k in "hl")
        wc2_h, wc2_l = (sb(f"wc2_{k}", [P, K2, P], F32R) for k in "hl")
        wp_pair = sb("wp_pair", [P, 2 * KS, P], F32R)
        wp_cross = sb("wp_cross", [P, K2, P], F32R)
        keep = sb("keep", [C, 2 * DUO * HW])
        r12 = x_t[:, 0:HALF, :].rearrange("p (b n) q -> p b n q", b=2)
        maxima = x_t[:, HALF:N, :].rearrange("p (b n) q -> p b n q", b=2)
        pool_pair = sb("pool_pair", [P, HALF, PW, PW], F32R)
        pool_cross = sb("pool_cross", [P, HALF, PW, PW], F32R)
        c_aff = x_b
        pre = comb_t[:, :, :].rearrange("p j q -> p (j q)").rearrange("p (n q) -> p n q", q=HW)
        g2_h, g2_l = (sb(f"g2_{k}", [P, HALF, PW, PW], F32R) for k in "hl")
        u_flat = u[:, :, :, :].rearrange("p k x h -> p (k x h)")
        res, whole, pool_whole = (u_flat[:, i * HALF * HW:(i + 1) * HALF * HW].rearrange("p (n q) -> p n q", q=HW)
                                  for i in range(3))

        bank = [ctx.enter_context(nc.psum_tensor(f"bank{i}", [P, 512], F32)) for i in range(8)]
        comb_bank, cell_bank, y0_banks = bank[4], bank[5], bank[6:8]

        ld_x = [sem(f"ld_x{i}") for i in range(2)]
        ld_xt = sem("ld_xt")
        ld_cst = sem("ld_cst")
        ld_w0 = [sem(f"ld_w0_{i}") for i in range(4)]
        ld_w12, ld_wp, ld_vec, ld_c = sem("ld_w12"), sem("ld_wp"), sem("ld_vec"), sem("ld_c")
        zeroed = sem("zeroed")
        bias_zero = sem("bias_zero")
        v_zero = sem("v_zero")
        w_high = sem("w_high")
        w_pair_ready = sem("w_pair_ready")
        w_split = sem("w_split")
        g_high = sem("g_high")
        g_low = sem("g_low")
        g_copied = sem("g_copied")
        step = sem("step")
        stats_in = sem("stats_in")
        stats_ps = sem("stats_ps")
        var_ready = sem("var_ready")
        rstd_ready = sem("rstd_ready")
        norm_ready = sem("norm_ready")
        g_zero = sem("g_zero")
        g_ready = sem("g_ready")
        v_ps = sem("v_ps")
        v_ready = sem("v_ready")
        v_moved = [sem(f"v_moved{i}") for i in range(ND)]
        off_ps = sem("off_ps")
        u_ready = sem("u_ready")
        mod_ready = sem("mod_ready")
        dist_done = sem("dist_done")
        far_test = sem("far_test")
        hat_ready = sem("hat_ready")
        hat_used = sem("hat_used")
        prod_ready = sem("prod_ready")
        tap_ps = sem("tap_ps")
        cell_ts = sem("cell_ts")
        cell_ps = sem("cell_ps")
        part_ready = sem("part_ready")
        part_used = sem("part_used")
        flag_in = sem("flag_in")
        flag_ps = sem("flag_ps")
        flag_sb = sem("flag_sb")
        comb_ts = sem("comb_ts")
        y0_ps = sem("y0_ps")
        g1_ready = sem("g1_ready")
        high = sem("high")
        low = sem("low")
        whole_ready = sem("whole_ready")
        g1_low = sem("g1_low")
        pool_low = sem("pool_low")
        pool_copied = sem("pool_copied")
        g2_low = sem("g2_low")
        r12_ps = sem("r12_ps")
        c_ps = sem("c_ps")
        r12_ready = sem("r12_ready")
        r12_used = sem("r12_used")
        pooled_ready = sem("pooled_ready")
        p_ps = sem("p_ps")
        caff_ready = sem("caff_ready")
        pre_ready = sem("pre_ready")
        g2_ready = sem("g2_ready")
        o_ps = sem("o_ps")
        relu_ready = sem("relu_ready")
        res_ready = sem("res_ready")
        stored = sem("stored")
        far_v0 = sem("far_v0")
        far_v = sem("far_v")
        far_row_done = sem("far_row_done")
        far_runs = sem("far_runs")
        far = sem("far")
        far_tp = sem("far_tp")
        far_ts = sem("far_ts")
        far_y = sem("far_y")
        far_added = sem("far_added")

        v_dram = nc.dram_tensor("v_rows", [P + 2 * (H - 1) * N, W * C], F32, kind="Internal").ap()

        block = ctx.enter_context(nc.Block())

        x_d = x.rearrange("n c h w -> n c (h w)")
        out_d = out.rearrange("n c h w -> n c (h w)")
        lo, hi = slice(0, C), slice(C, P)

        def inner(tile, n0, n, part=slice(0, P)):
            return tile[part, n0:n0 + n, 1:H + 1, 1:W + 1]

        def rows_cols(ap):
            return ap.rearrange("p (y x) -> p y x", x=W)

        def pair_stats(s):
            b = {G_IN: 5, G_IN + 1: 4, G_C1: 7, G_P: 7, G_C1 + 2: 2, G_P + 2: 7}[s]
            return bank[b][:, 0:2 * DUO]

        def cell_blocks(c, g):
            q0, q1, _ = GROUPS[g]
            cols = (q1 - q0) * CHUNKS[c][1] * HEADS
            n = -(-cols // P)
            return n, cols // n, 2 * g, bank[(2, 3, 2)[g]]

        def cells_ps(c, i):
            cx = CHUNKS[c][1] * HEADS
            if CELL0[i] >= GROUPS[-1][0]:
                return bank[3][:, 2 * P:2 * P + 3 * cx]
            return cell_bank[:, CELL0[i] * cx:(CELL0[i] + 5) * cx]

        OUT_PARTS = ((0, DUO), (DUO, 1), (DUO + 1, 1))
        out_banks = (bank[6], bank[7], bank[0])

        @block.sync
        def _(sp):
            sp.dma_start(x_b[lo, :, :], x_d[0:HALF].rearrange("n c p -> c n p")).then_inc(ld_x[0], 16)
            sp.dma_start(cst[:, :], consts).then_inc(ld_cst, 16)
            sp.dma_start(w_raw[lo], w_off).then_inc(ld_w0[1], 16)
            sp.dma_start(x_t, x_d.rearrange("n c p -> c n p")).then_inc(ld_xt, 16)
            sp.wait_ge(bias_zero, 1)
            for row in (0, LO_ROW):
                sp.dma_start(bias_s[row:row + 1, :], off_bias).then_inc(ld_w0[2], 16)
            for rows in (lo, hi):
                sp.dma_start(w_v_s[rows, :], w_v).then_inc(ld_w0[0], 16)
            sp.dma_start(w_o_s[:, :], w_o).then_inc(ld_w0[3], 16)
            sp.dma_start(vec_s[:, :], vecs).then_inc(ld_vec, 16)
            sp.dma_start(b12_s[:, :], b12).then_inc(ld_vec, 16)
            sp.wait_ge(v_ready, 1)
            for i in (4, 1, 3, 0):
                d = (i - WIN) * N
                dst, src = (slice(0, P - d), slice(d, P)) if d > 0 else (slice(-d, P), slice(0, P + d))
                sp.dma_start(v[dst, i, WIN:WIN + W, :], v[src, WIN, WIN:WIN + W, :]).then_inc(v_moved[i], 16)
            sp.wait_ge(zeroed, 3)
            for b in range(2):
                for half in range(2):
                    cols = slice(b * C + half * CD, b * C + (half + 1) * CD)
                    sp.dma_start(raw[half * C:(half + 1) * C, 0, :, cols], w12[b]).then_inc(ld_w12, 16)
            for half in range(2):
                rows = slice(half * C, (half + 1) * C)
                sp.dma_start(raw_c1[rows, rows], wc1).then_inc(ld_c, 16)
                sp.dma_start(raw[rows, 1, :, rows], wc2).then_inc(ld_c, 16)
            sp.wait_ge(zeroed, 6)
            for copy in range(2):
                for half in range(2):
                    rows = slice(copy * C + half * CD, copy * C + (half + 1) * CD)
                    sp.dma_start(raw[rows, 0, :, half * C:(half + 1) * C], wp).then_inc(ld_wp, 16)
            sp.wait_ge(flag_sb, 1)
            count = sp.value_load(vcount[0:1, 0:1], min_val=0, max_val=2 * NC * P)
            with sp.If(count > 0):
                sp.wait_ge(far_row_done, 1)
                pad = (H - 1) * N
                flat = vfar[:, 0:W, :].rearrange("p x c -> p (x c)")
                sp.dma_start(v_dram[0:pad, :], flat[0:pad, :]).then_inc(far_v0, 16)
                sp.dma_start(v_dram[pad + P:, :], flat[0:pad, :]).then_inc(far_v0, 16)
                sp.dma_start(v_dram[pad:pad + P, :],
                             v[:, WIN, WIN:WIN + W, :].rearrange("p x c -> p (x c)")).then_inc(far_v0, 16)
                sp.wait_ge(far_v0, 48)
                with sp.Fori(0, FULL) as k:
                    sp.wait_ge(far_row_done, k + 1)
                    sp.dma_start(vfar[:, PADX:PADX + W, :].rearrange("p x c -> p (x c)"),
                                 v_dram[bass.ds(k * N, P), :]).then_inc(far_v, 16)
            for j, (i0, n) in enumerate(OUT_PARTS):
                sp.wait_ge(res_ready, j + 1)
                sp.dma_start(out_d[i0:i0 + n].rearrange("n c p -> c n p"), res[lo, i0:i0 + n, :]).then_inc(stored, 16)
            sp.wait_ge(stored, 2 * 16 * len(OUT_PARTS))

        @block.gpsimd
        def _(pool):
            nc.gpsimd.memset(ones[:, :], 1.0).then_inc(zeroed, 1)
            nc.gpsimd.memset(bias_s[:, :], 0.0).then_inc(bias_zero, 1)
            nc.gpsimd.memset(half_pow[:, :], -0.5)
            nc.gpsimd.memset(g_pair[:, PW - 1, :, :].bitcast(F32), 0.0)
            nc.gpsimd.memset(ones_r[:, :].bitcast(F32), 1.0)
            nc.gpsimd.memset(w_v_pair[:, :].bitcast(F32), 0.0)
            nc.gpsimd.memset(w_pair[:, 1::2, :].bitcast(F32), 0.0).then_inc(zeroed, 1)
            nc.gpsimd.memset(v[:, :, :, :], 0.0).then_inc(v_zero, 1)

            def rstd(s, cols):
                pool.wait_ge(var_ready, s + 1)
                nc.gpsimd.tensor_tensor(ab[:, s, 2, 0:cols], ab[:, s, 1, 0:cols], half_pow[:, 0:cols],
                                        ALU.pow).then_inc(rstd_ready, 1)

            pool.wait_ge(zeroed, 2)
            rstd(G0, N)
            pool.wait_ge(w_high, 1)
            pool.wait_ge(rstd_ready, 1)
            nc.gpsimd.tensor_tensor(w_cross[hi, :, :], w_raw[hi], w_cross[hi, :, :].bitcast(F32),
                                    ALU.subtract).then_inc(w_split, 1)
            pool.wait_ge(w_split, 1)
            pool.wait_ge(w_high, 2)
            row = slice(LO_ROW, LO_ROW + 1)
            nc.gpsimd.tensor_tensor(bias_r[row, :], bias_s[row, :], bias_r[row, :].bitcast(F32),
                                    ALU.subtract).then_inc(w_split, 1)
            pool.wait_ge(w_split, 2)
            pool.wait_ge(g_ready, N)
            nc.gpsimd.memset(raw_c1[:, :], 0.0)
            nc.gpsimd.memset(staging[:, :], 0.0).then_inc(zeroed, 1)
            pool.wait_ge(off_ps, NC)
            nc.gpsimd.memset(keep[:, :], 1.0).then_inc(zeroed, 1)
            pool.wait_ge(zeroed, 4)
            nc.gpsimd.memset(keep[:, :].rearrange("p (r i) -> p r i", i=W)[:, :, W - 1:W], 0.0)
            nc.gpsimd.memset(wp_pair[:, :, :].bitcast(F32), 0.0)
            for padded in (g1_h, g1_l, pool_pair, pool_cross, g2_h, g2_l):
                last = nc.gpsimd.memset(padded[:, :, :, :].bitcast(F32), 0.0)
            last.then_inc(zeroed, 1)
            pool.wait_ge(high, 1)
            nc.gpsimd.tensor_tensor(w12_l[:, :, :], raw[:, 0], w12_h[:, :, :].bitcast(F32),
                                    ALU.subtract).then_inc(low, 1)
            pool.wait_ge(low, 1)
            nc.gpsimd.memset(raw[:, 0], 0.0).then_inc(zeroed, 1)
            pool.wait_ge(high, 3)
            nc.gpsimd.tensor_tensor(wc1_l[:, :], raw_c1[:, :], wc1_h[:, :].bitcast(F32),
                                    ALU.subtract).then_inc(low, 1)
            nc.gpsimd.tensor_tensor(wc2_l[:, :, :], raw[:, 1], wc2_h[:, :, :].bitcast(F32),
                                    ALU.subtract).then_inc(low, 1)
            pool.wait_ge(high, 4)
            pool.wait_ge(low, 3)
            nc.gpsimd.tensor_tensor(wp_cross[hi, :, :], raw[hi, 0], wp_cross[hi, :, :].bitcast(F32),
                                    ALU.subtract).then_inc(low, 1)
            pool.wait_ge(low, 4)
            for s in range(G_IN, NORMS):
                rstd(s, DUO)

        DVE_IMAGES = 5

        @block.scalar
        def _(act):
            act.dma_start(x_b[hi, :, :], x_d[HALF:N].rearrange("n c p -> c n p")).then_inc(ld_x[1], 16)
            act.dma_start(w_raw[hi], w_off).then_inc(ld_w0[1], 16)
            act.wait_ge(zeroed, 1)
            nc.scalar.activation(warm[:, :], ones[:, :], ACT.Sigmoid)
            act.wait_ge(ld_w0[1], 32)
            nc.scalar.activation(w_cross[:, :, :], w_raw, ACT.Copy).then_inc(w_high, 1)
            act.wait_ge(ld_xt, 16)
            act.wait_ge(g_zero, 1)
            act.wait_ge(norm_ready, 1)
            for n in range(DVE_IMAGES, N):
                nc.scalar.activation(g_t[:, 1:W + 1, 1:H + 1, n].rearrange("p x y -> p y x"), rows_cols(x_t[:, n, :]),
                                     ACT.Identity, bias=ab[lo, G0, 3, n:n + 1],
                                     scale=ab[lo, G0, 2, n:n + 1]).then_inc(g_ready, 1)

            def copy_high(r):
                act.wait_ge(g_high, r + 1)
                xa, xb = RANGES[r]
                xl = max(xa, 1)
                nc.scalar.activation(g_pair[hi, xl - 1:xb - 1], g_pair[lo, xl:xb], ACT.Copy)
                nc.scalar.activation(g_cross[hi, xa:xb], g_pair[lo, xa:xb], ACT.Copy).then_inc(g_copied, 1)

            act.wait_ge(ld_w0[2], 32)
            nc.scalar.activation(bias_r[:, :], bias_s[:, :], ACT.Copy).then_inc(w_high, 1)
            copy_high(0)
            nc.scalar.activation(w_pair[hi, 0::2, :], w_raw[hi, 1::KS, :], ACT.Copy).then_inc(w_high, 1)
            copy_high(1)

            def copy_values():
                act.wait_ge(v_zero, 1)
                act.wait_ge(v_ps, 1)
                for b in range(4):
                    last = nc.scalar.activation(v[:, WIN, WIN + 4 * b:WIN + 4 * (b + 1), :],
                                                bank[4 + b][:, :].rearrange("p (x q) -> p x q", q=P)[:, :, 0:C],
                                                ACT.Copy)
                last.then_inc(v_ready, 1)

            def copy_offsets(c):
                x0 = CHUNKS[c][0]
                act.wait_ge(off_ps, c + 1)
                for b, k in enumerate(CONV_BANKS[c]):
                    xa = x0 + 2 * b
                    last = nc.scalar.activation(u[:, :, xa:xa + 2, :].rearrange("p k x h -> p x k h"),
                                                bank[k][:, 0:2 * NCH].rearrange("p (x k h) -> p x k h", x=2, h=HEADS),
                                                ACT.Copy)
                last.then_inc(u_ready, 1)

            def distances(c, d0, d1):
                x0, w = CHUNKS[c]
                ck = K2 * w * HEADS
                xs = slice(x0, x0 + w)
                act.wait_ge(u_ready, c + 1)
                if d0 == 0:
                    nc.scalar.activation(mod[:, :, xs, :], u[:, 2 * K2:, xs, :], ACT.Sigmoid).then_inc(mod_ready, 1)
                    if c >= 2:
                        act.wait_ge(hat_used, c - 1)
                for d in range(d0, d1):
                    nc.scalar.activation(
                        hat[:, c % 2, d, 0:2 * ck].rearrange("p (k x h) -> p k x h", x=w, h=HEADS),
                        u[:, 0:2 * K2, xs, :], ACT.Abs, bias=float(WIN - d), scale=STEP).then_inc(dist_done, 1)

            def hats(c):
                ck = K2 * CHUNKS[c][1] * HEADS
                act.wait_ge(dist_done, ND * (c + 1))
                nc.scalar.activation(beyond[:, 0:2 * ck], hat[:, c % 2, WIN, 0:2 * ck], ACT.Relu, bias=-float(WIN),
                                     accum_out=vfar_sum[:, c:c + 1]).then_inc(far_test, 1)
                act.wait_ge(far_test, c + 1)
                nc.scalar.activation(hat[:, c % 2, :, 0:2 * ck], hat[:, c % 2, :, 0:2 * ck], ACT.Relu, bias=1.0,
                                     scale=-1.0).then_inc(hat_ready, 1)

            def copy_sums(c, g):
                n, size, b0, bank_ps = cell_blocks(c, g)
                act.wait_ge(tap_ps, len(GROUPS) * c + g + 1)
                if c:
                    act.wait_ge(cell_ps, len(GROUPS) * (c - 1) + g + 1)
                nc.scalar.activation(cell_t[0:size, b0:b0 + n, :],
                                     bank_ps[0:size, 0:n * P].rearrange("p (b q) -> p b q", q=P),
                                     ACT.Copy).then_inc(cell_ts, 1)

            def evacuate(c):
                x0, w = CHUNKS[c]
                act.wait_ge(part_used, ND * (c + 1))
                nc.scalar.activation(comb_t[:, x0 // 2:(x0 + w) // 2, :],
                                     comb_bank[:, 0:w * C].rearrange("p (j q) -> p j q", q=P),
                                     ACT.Copy).then_inc(comb_ts, 1)

            copy_high(2)
            copy_offsets(0)
            distances(0, 0, ND)
            hats(0)
            copy_values()
            copy_offsets(1)
            distances(1, 0, 1)
            for c in range(NC):
                if c:
                    evacuate(c - 1)
                    if c + 1 < NC:
                        distances(c + 1, 0, 1)
                for g in range(len(GROUPS)):
                    copy_sums(c, g)
                    if c + 1 < NC:
                        distances(c + 1, g + 1, g + 2)
                if c + 1 < NC:
                    distances(c + 1, ND - 1, ND)
                    hats(c + 1)
                if c + 2 < NC:
                    copy_offsets(c + 2)
                if c == NC - 2:
                    act.wait_ge(ld_w12, 64)
                    nc.scalar.activation(w12_h[:, :, :], raw[:, 0], ACT.Copy).then_inc(high, 1)
                    act.wait_ge(ld_c, 64)
                    nc.scalar.activation(wc1_h[:, :], raw_c1[:, :], ACT.Copy).then_inc(high, 1)
                    nc.scalar.activation(wc2_h[:, :, :], raw[:, 1], ACT.Copy).then_inc(high, 1)
                if c == NC - 1:
                    act.wait_ge(ld_wp, 64)
                    act.wait_ge(zeroed, 5)
                    nc.scalar.activation(wp_cross[:, :, :], raw[:, 0], ACT.Copy).then_inc(high, 1)
                    for rows, kx, single in ((lo, 0, 0), (hi, 1, 0), (lo, 2, 1)):
                        nc.scalar.activation(wp_pair[rows, single::2, :], raw[rows, 0, kx::KS, :],
                                             ACT.Copy).then_inc(high, 1)
            evacuate(NC - 1)

            act.wait_ge(zeroed, 5)
            for g in range(2):
                act.wait_ge(norm_ready, G_IN + g + 1)
                for j in range(DUO):
                    n = DUO * g + j
                    nc.scalar.activation(inner(g1_h, n, 1)[:, 0], rows_cols(x1[:, n, :]), ACT.Identity,
                                         bias=ab[:, G_IN + g, 3, j:j + 1],
                                         scale=ab[:, G_IN + g, 2, j:j + 1]).then_inc(g1_ready, 1)

            def affine_c(g):
                act.wait_ge(norm_ready, G_C1 + 2 * g + 1)
                for j in range(DUO):
                    last = nc.scalar.activation(c_aff[:, DUO * g + j, :], bank[2 + g][:, j * HW:(j + 1) * HW],
                                                ACT.Identity, bias=ab[:, G_C1 + 2 * g, 3, j:j + 1],
                                                scale=ab[:, G_C1 + 2 * g, 2, j:j + 1])
                last.then_inc(caff_ready, 1)

            act.wait_ge(ld_vec, 32)
            for g in range(2):
                act.wait_ge(r12_ps, g + 1)
                if g:
                    act.wait_ge(r12_used, 1)
                nc.scalar.activation(r12[:, 0].rearrange("p n (x y) -> p n y x", y=H),
                                     bank[g][lo, :].rearrange("p (n y x) -> p n y x", n=DUO, x=W), ACT.Relu,
                                     bias=b12_s[lo, 0:1])
                nc.scalar.activation(r12[:, 1], bank[g][hi, :].rearrange("p (n q) -> p n q", n=DUO), ACT.Relu,
                                     bias=b12_s[hi, 0:1]).then_inc(r12_ready, 1)
                if g:
                    affine_c(0)
                act.wait_ge(pooled_ready, g + 1)
                nc.scalar.activation(inner(pool_cross, DUO * g, DUO, hi), inner(pool_pair, DUO * g, DUO, lo),
                                     ACT.Copy).then_inc(pool_copied, 1)
            for g in range(2):
                if g:
                    affine_c(g)
                for j in range(DUO):
                    n = DUO * g + j
                    act.wait_ge(pre_ready, n + 1)
                    nc.scalar.activation(inner(g2_h, n, 1)[:, 0], rows_cols(pre[:, n, :]), ACT.Relu,
                                         bias=ab[:, G_P + 2 * g, 3, j:j + 1]).then_inc(g2_ready, 1)
            for k, (i0, n) in enumerate(OUT_PARTS):
                act.wait_ge(o_ps, k + 1)
                nc.scalar.activation(res[:, i0:i0 + n, :], out_banks[k][:, 0:n * HW].rearrange("p (n q) -> p n q", n=n),
                                     ACT.Relu, bias=vec_s[:, 4:5]).then_inc(relu_ready, 1)
            for k, (i0, n) in enumerate(OUT_PARTS):
                act.wait_ge(res_ready, k + 1)
                act.dma_start(out_d[HALF + i0:HALF + i0 + n].rearrange("n c p -> c n p"),
                              res[hi, i0:i0 + n, :]).then_inc(stored, 16)

        @block.vector
        def _(ve):
            steps = [0]

            def tick(ins):
                steps[0] += 1
                ins.then_inc(step, 1)
                return steps[0]

            def link(ins):
                ve.wait_ge(step, tick(ins))

            def norm_stats(s, views):
                cols = len(views)
                for n, view in enumerate(views):
                    last = nc.vector.bn_stats(bn[:, s, n, :], view)
                link(last)
                for n in range(cols):
                    last = nc.vector.bn_aggr(mv[:, s, n, :], bn[:, s, n, :])
                link(last)
                link(nc.vector.tensor_tensor(sq[:, s, 0:cols], mv[:, s, 0:cols, 0], mv[:, s, 0:cols, 0], ALU.mult))
                nc.vector.tensor_tensor(mv[:, s, 0:cols, 1], mv[:, s, 0:cols, 1], sq[:, s, 0:cols],
                                        ALU.add).then_inc(stats_in, 1)

            def variance(s, cols, stat):
                ve.wait_ge(stats_ps, s + 1)
                link(nc.vector.tensor_copy(ab[:, s, 0:2, 0:cols], stat.rearrange("p (n t) -> p t n", t=2)))
                link(nc.vector.tensor_tensor(sq[:, s, 0:cols], ab[:, s, 0, 0:cols], ab[:, s, 0, 0:cols], ALU.mult))
                nc.vector.scalar_tensor_tensor(ab[:, s, 1, 0:cols], ab[:, s, 1, 0:cols], EPS, sq[:, s, 0:cols],
                                               ALU.add, ALU.subtract).then_inc(var_ready, 1)

            def affine(s, cols, gamma=None, beta=None, extra=None):
                ve.wait_ge(rstd_ready, s + 1)
                scale, shift = ab[:, s, 2, 0:cols], ab[:, s, 3, 0:cols]
                if gamma is not None:
                    link(nc.vector.tensor_scalar(scale, scale, gamma, None, ALU.mult))
                ins = nc.vector.scalar_tensor_tensor(shift, ab[:, s, 0, 0:cols], -1.0, scale, ALU.mult, ALU.mult)
                if beta is not None:
                    link(ins)
                    ins = nc.vector.tensor_scalar(shift, shift, beta, extra, ALU.add, ALU.add)
                ins.then_inc(norm_ready, 1)

            def far_displacements():
                def wait(n):
                    ve.wait_ge(far, n)

                def run(base, steps):
                    for j, ins in enumerate(steps):
                        ins().then_inc(far, 1)
                        wait(base + j + 1)
                    ve.sem_inc(far_runs, 1)
                    return base + len(steps)

                ux = u[:, 0:K2, :, :].rearrange("p k x h -> p k (x h)")
                uy = u[:, K2:2 * K2, :, :].rearrange("p k x h -> p k (x h)")
                m = mod[:, :, :, :].rearrange("p k x h -> p k (x h)")
                middle = vfar[:, PADX:PADX + W, :]

                def hat_steps(a, src, i):
                    t = fdist[:, a]
                    ramp = cst[:, bass.ds(C_RAMP + i, 1)]
                    return [lambda: nc.vector.tensor_copy(fmove[:, :], ramp),
                            lambda: nc.vector.tensor_scalar(t, src, STEP, fmove[:, 0:1], ALU.mult, ALU.subtract),
                            lambda: nc.vector.scalar_tensor_tensor(t, t, -1.0, t, ALU.mult, ALU.min),
                            lambda: nc.vector.tensor_scalar(t, t, 1.0, 0.0, ALU.add, ALU.max)]

                def row_steps(i):
                    return hat_steps(1, uy, i) + [
                        lambda: nc.vector.tensor_tensor(fdist[:, 1], fdist[:, 1], m, ALU.mult)]

                def cell_steps(i):
                    return hat_steps(0, ux, i) + [
                        lambda: nc.vector.tensor_tensor(fprod, fdist[:, 0], fdist[:, 1], ALU.mult),
                        lambda: nc.vector.tensor_reduce(fcell[:, :], fprod.rearrange("p k q -> p q k"),
                                                        AX_X, ALU.add),
                        lambda: nc.vector.tensor_tensor(
                            fpart.rearrange("p x (h e) -> p (x h) e", e=HD),
                            vfar[:, bass.ds(i, W), :].rearrange("p x (h e) -> p (x h) e", e=HD),
                            fcell[:, :].unsqueeze(2).to_broadcast([P, W * HEADS, HD]), ALU.mult),
                        lambda: nc.vector.tensor_tensor(far_sum, far_sum, fpart, ALU.add)]

                CELL = 8

                def columns(base, i0, i1):
                    with ve.Fori(i0, i1) as i:
                        run(base + (i - i0) * CELL, cell_steps(i))
                    return base + (i1 - i0) * CELL

                ve.wait_ge(part_used, ND * NC)
                n = run(0, [lambda: nc.vector.memset(vfar[:, :, :], 0.0),
                            lambda: nc.vector.memset(far_sum, 0.0)])
                ve.sem_inc(far_row_done, 1)
                for r0, r1, ranges in FAR_ROWS:
                    per_row = 5 + sum(i1 - i0 for i0, i1 in ranges) * CELL
                    with ve.Fori(r0, r1) as k:
                        base = n + (k - r0) * per_row
                        ve.wait_ge(far_v, (k + 1) * 16)
                        base = run(base, row_steps(k))
                        for i0, i1 in ranges:
                            base = columns(base, i0, i1)
                        ve.sem_inc(far_row_done, 1)
                    n += per_row * (r1 - r0)
                ve.sem_inc(far_ts, 1)
                ve.wait_ge(far_tp, 1)
                for b in range(2):
                    last = nc.vector.tensor_copy(far_t[:, b * W // 4:(b + 1) * W // 4, :],
                                                 bank[b][:, :].rearrange("p (j q) -> p j q", q=P))
                last.then_inc(far_ts, 1)
                ve.wait_ge(far_y, 1)
                for par in range(2):
                    t = x_b[:, :, :].rearrange("p n (y j a) -> p a j y n", a=2, j=W // 2)[:, par]
                    nc.vector.tensor_tensor(t, bank[2 + par][:, :].rearrange("p (j y n) -> p j y n", y=H, n=HALF), t,
                                            ALU.add).then_inc(far_added, 1)
                ve.wait_ge(far_added, 2)

            nc.vector.memset(g_t[:, :, :, :], 0.0).then_inc(g_zero, 1)
            for half in range(2):
                ve.wait_ge(ld_x[half], 16)
            norm_stats(G0, [x_b[:, n, :] for n in range(HALF)])
            variance(G0, N, bank[7][:, 0:2 * N])
            affine(G0, N)
            ve.wait_ge(norm_ready, 1)
            ve.wait_ge(ld_xt, 16)
            ve.wait_ge(g_zero, 1)
            for n in range(DVE_IMAGES):
                nc.vector.tensor_scalar(g_t[:, 1:W + 1, 1:H + 1, n].rearrange("p x y -> p y x"),
                                        rows_cols(x_t[:, n, :]), ab[lo, G0, 2, n:n + 1], ab[lo, G0, 3, n:n + 1],
                                        ALU.mult, ALU.add).then_inc(g_ready, 1)
            ve.wait_ge(g_ready, N)
            ve.wait_ge(zeroed, 2)
            for r, (xa, xb) in enumerate(RANGES):
                nc.vector.tensor_copy(g_pair[lo, xa:xb], g_t[:, xa:xb]).then_inc(g_high, 1)
                ve.wait_ge(g_high, r + 1)
                nc.vector.tensor_tensor(g_cross[lo, xa:xb], g_t[:, xa:xb], g_pair[lo, xa:xb].bitcast(F32),
                                        ALU.subtract).then_inc(g_low, 1)
                if r == 0:
                    ve.wait_ge(ld_w0[1], 32)
                    for kx, single in ((0, 0), (2, 1)):
                        nc.vector.tensor_copy(w_pair[lo, single::2, :], w_raw[lo, kx::KS, :]).then_inc(w_pair_ready, 1)
            ve.wait_ge(ld_w0[0], 32)
            nc.vector.tensor_copy(w_v_pair[lo, :], w_v_s[lo, :])
            link(nc.vector.tensor_copy(w_v_cross[:, :], w_v_s[:, :]))
            nc.vector.tensor_tensor(w_v_cross[hi, :], w_v_s[hi, :], w_v_cross[hi, :].bitcast(F32),
                                    ALU.subtract).then_inc(w_pair_ready, 1)

            applied = [0]

            def chunk(c):
                x0, w = CHUNKS[c]
                cx = w * HEADS
                ck = K2 * cx
                cv = w * C

                def product(i):
                    nd, d0, q0 = 2 * DX[i] + 1, WIN - DX[i], CELL0[i]
                    return nc.vector.tensor_tensor(
                        prod[:, 0:K2 * CELLS * cx].rearrange("p (k q s) -> p q k s", k=K2, s=cx)[:, q0:q0 + nd],
                        hat[:, c % 2, d0:d0 + nd, 0:ck].rearrange("p d (k s) -> p d k s", s=cx),
                        wy[:, i:i + 1, 0:ck].rearrange("p d (k s) -> p d k s", s=cx).to_broadcast([P, nd, K2, cx]),
                        ALU.mult)

                def apply(i):
                    nd = 2 * DX[i] + 1
                    n = applied[0]
                    applied[0] += 1
                    if c == 0:
                        if i == WIN:
                            ve.wait_ge(v_ready, 1)
                        else:
                            ve.wait_ge(v_moved[i], 16)
                    if n >= PARTS:
                        ve.wait_ge(part_used, n - PARTS + 1)
                    if i == OWN_ROW:
                        ve.wait_ge(step, own_sum)
                        weights = cell[:, 0:nd, 0:cx]
                    else:
                        last_group = CELL0[i] >= GROUPS[-1][0]
                        ve.wait_ge(cell_ps, len(GROUPS) * c + (3 if last_group else 2))
                        weights = cells_ps(c, i).rearrange("p (d q) -> p d q", d=nd)
                    xa = x0 + WIN - DX[i]
                    v0 = v[:, i, xa:xa + w, :]
                    moved = bass.AP(v0.tensor, v0.offset, [v0.ap[0], [C, nd], [HD, cx], [1, HD]])
                    nc.vector.tensor_tensor(part[:, n % PARTS, 0:nd, 0:cv].rearrange("p d (q e) -> p d q e", e=HD),
                                            moved, weights.unsqueeze(3).to_broadcast([P, nd, cx, HD]),
                                            ALU.mult).then_inc(part_ready, 1)

                ve.wait_ge(hat_ready, c + 1)
                ve.wait_ge(mod_ready, c + 1)
                if c:
                    ve.wait_ge(step, last_made[0])
                made_wy = tick(nc.vector.tensor_tensor(
                    wy[:, :, 0:ck].rearrange("p d (k q) -> p d k q", k=K2),
                    hat[:, c % 2, :, ck:2 * ck].rearrange("p d (k q) -> p d k q", k=K2),
                    mod[:, :, x0:x0 + w, :].rearrange("p k x h -> p k (x h)").unsqueeze(1).to_broadcast(
                        [P, ND, K2, cx]), ALU.mult))
                nc.vector.tensor_tensor_reduce(out=edge[:, 0:ck], in0=hat[:, c % 2, WIN, 0:ck],
                                               in1=hat[:, c % 2, WIN, ck:2 * ck], scale=1.0, scalar=2.0,
                                               op0=ALU.add, op1=ALU.min, accum_out=vmin[:, c:c + 1])
                ve.wait_ge(step, made_wy)
                for i in ROWS[:-1]:
                    product(i).then_inc(prod_ready, 1)
                product(OWN_ROW).then_inc(hat_used, 1)
                ve.wait_ge(hat_used, c + 1)
                if c == NC - 1:
                    window_test()
                q0 = CELL0[OWN_ROW]
                own_sum = tick(nc.vector.tensor_reduce(
                    cell[:, :, 0:cx],
                    prod[:, 0:K2 * CELLS * cx].rearrange("p (k q s) -> p q s k", k=K2, s=cx)[:, q0:q0 + 3], AX_X,
                    ALU.add))
                for i in APPLY[:-1]:
                    apply(i)
                if c == NC - 1:
                    ve.wait_ge(flag_ps, 1)
                    link(nc.vector.tensor_reduce(vtotal[:, :], bank[1][0:1, 0:2 * NC], AX_X, ALU.add))
                    nc.vector.tensor_copy(vcount[:, :], vtotal[:, :]).then_inc(flag_sb, 1)
                apply(APPLY[-1])

            def window_test():
                ve.wait_ge(far_test, NC)
                nc.vector.tensor_scalar(vflag[:, 0, :], vmin[:, :], 0.0, None, ALU.is_le)
                nc.vector.tensor_scalar(vflag[:, 1, :], vfar_sum[:, :], 0.0, None, ALU.is_gt).then_inc(flag_in, 1)

            last_made = [0]
            for c in range(NC):
                chunk(c)
                last_made[0] = steps[0]
            ve.wait_ge(flag_sb, 1)
            count = ve.value_load(vcount[0:1, 0:1], min_val=0, max_val=2 * NC * P)
            with ve.If(count > 0):
                far_displacements()

            ve.wait_ge(y0_ps, NC)

            def residual(g):
                n0 = DUO * g
                for par in range(2):
                    def column_pairs(t):
                        return t[:, n0:n0 + DUO, :].rearrange("p n (y j a) -> p a j y n", a=2, j=W // 2)[:, par]
                    last = nc.vector.tensor_tensor(
                        column_pairs(x1), y0_banks[par][:, :].rearrange("p (j y n) -> p j y n", y=H, n=HALF)[
                            :, :, :, n0:n0 + DUO], column_pairs(x_b), ALU.add)
                return tick(last)

            def x1_stats(g, added):
                ve.wait_ge(step, added)
                norm_stats(G_IN + g, [x1[:, DUO * g + j, :] for j in range(DUO)])

            def low_parts(n0, n, high_tile, make, high_ready, done):
                for i in range(n0, n0 + n):
                    make(i, whole[:, i, :]).then_inc(whole_ready, 1)
                    wholes[0] += 1
                    ve.wait_ge(whole_ready, wholes[0])
                    ve.wait_ge(high_ready, i + 1)
                    padded_low, padded_high = (inner(t, i, 1)[:, 0] for t in high_tile)
                    nc.vector.tensor_tensor(padded_low, rows_cols(whole[:, i, :]), padded_high.bitcast(F32),
                                            ALU.subtract).then_inc(done, 1)

            wholes = [0]

            def g1_low_parts(g):
                ve.wait_ge(norm_ready, G_IN + g + 1)
                low_parts(DUO * g, DUO, (g1_l, g1_h), lambda i, dst: nc.vector.tensor_scalar(
                    dst, x1[:, i, :], ab[:, G_IN + g, 2, i % DUO:i % DUO + 1],
                    ab[:, G_IN + g, 3, i % DUO:i % DUO + 1], ALU.mult, ALU.add), g1_ready, g1_low)

            x1_stats(0, residual(0))
            variance(G_IN, DUO, pair_stats(G_IN))
            added = residual(1)
            affine(G_IN, DUO)
            x1_stats(1, added)
            ve.wait_ge(zeroed, 5)
            g1_low_parts(0)
            variance(G_IN + 1, DUO, pair_stats(G_IN + 1))
            affine(G_IN + 1, DUO)
            g1_low_parts(1)

            def c1_stats(g):
                ve.wait_ge(c_ps, g + 1)
                norm_stats(G_C1 + 2 * g, [bank[2 + g][:, j * HW:(j + 1) * HW] for j in range(DUO)])

            def reverse(ap):
                n = ap.ap[-1][1]
                return bass.AP(ap.tensor, ap.offset + n - 1, [ap.ap[0], [-1, n]])

            def pools(g):
                ve.wait_ge(r12_ready, g + 1)
                flat_in = r12.rearrange("p b n q -> p (b n q)")
                flat_out = maxima.rearrange("p b n q -> p (b n q)")
                ins = nc.vector.tensor_tensor_scan(reverse(flat_out), reverse(keep[:, :]), reverse(flat_in), 0.0,
                                                   ALU.mult, ALU.max)
                ins.then_inc(r12_used, 1)
                ve.wait_ge(r12_used, g + 1)
                top = maxima[:, 0].rearrange("p n (x y) -> p n y x", y=H)
                left = maxima[:, 1].rearrange("p n (y x) -> p n y x", x=W)
                n0 = DUO * g
                nc.vector.tensor_tensor(inner(pool_pair, n0, DUO, lo), top, left, ALU.add)
                nc.vector.tensor_tensor(pool_pair[hi, n0:n0 + DUO, 1:H + 1, 0:W], top, left,
                                        ALU.add).then_inc(pooled_ready, 1)
                sums = pool_whole[lo, n0:n0 + DUO].rearrange("p n (y x) -> p n y x", x=W)
                nc.vector.tensor_tensor(sums, top, left, ALU.add).then_inc(whole_ready, 1)
                wholes[0] += 1
                ve.wait_ge(whole_ready, wholes[0])
                nc.vector.tensor_tensor(inner(pool_cross, n0, DUO, lo), sums,
                                        inner(pool_pair, n0, DUO, lo).bitcast(F32), ALU.subtract).then_inc(pool_low, 1)

            ve.wait_ge(ld_vec, 32)

            def p_stats(g):
                ve.wait_ge(p_ps, g + 1)
                norm_stats(G_P + 2 * g, [bank[4 + g][:, j * HW:(j + 1) * HW] for j in range(DUO)])

            def c1_norm(g):
                variance(G_C1 + 2 * g, DUO, pair_stats(G_C1 + 2 * g))
                affine(G_C1 + 2 * g, DUO, vec_s[:, 2:3], vec_s[:, 3:4], vec_s[:, 1:2])

            def both_branches(g):
                s = G_P + 2 * g
                variance(s, DUO, pair_stats(s))
                affine(s, DUO, vec_s[:, 0:1])
                ve.wait_ge(norm_ready, s + 1)
                ve.wait_ge(caff_ready, g + 1)
                for j in range(DUO):
                    nc.vector.scalar_tensor_tensor(pre[:, DUO * g + j, :], bank[4 + g][:, j * HW:(j + 1) * HW],
                                                   ab[:, s, 2, j:j + 1], c_aff[:, DUO * g + j, :], ALU.mult,
                                                   ALU.add).then_inc(pre_ready, 1)

            def g2_low_parts(g):
                ve.wait_ge(pre_ready, DUO * (g + 1))
                low_parts(DUO * g, DUO, (g2_l, g2_h), lambda i, dst: nc.vector.tensor_scalar(
                    dst, pre[:, i, :], ab[:, G_P + 2 * g, 3, i % DUO:i % DUO + 1], 0.0, ALU.add, ALU.max),
                          g2_ready, g2_low)

            c1_stats(0)
            pools(0)
            c1_norm(0)
            pools(1)
            p_stats(0)
            both_branches(0)
            c1_stats(1)
            g2_low_parts(0)
            p_stats(1)
            c1_norm(1)
            both_branches(1)
            g2_low_parts(1)
            for k, (i0, n) in enumerate(OUT_PARTS):
                ve.wait_ge(relu_ready, k + 1)
                nc.vector.tensor_tensor(res[:, i0:i0 + n, :], res[:, i0:i0 + n, :], x1[:, i0:i0 + n, :],
                                        ALU.add).then_inc(res_ready, 1)

        @block.tensor
        def _(pe):
            ident = cst[:, C_ID:C_ID + P]

            def group_means(s, cols, out_ap, mats):
                pe.wait_ge(stats_in, s + 1)
                for i, m in enumerate(mats):
                    last = nc.tensor.matmul(out_ap[:, 2 * cols * i:2 * cols * (i + 1)], cst[:, m:m + P],
                                            mv[:, s, 0:cols, :].rearrange("p n t -> p (n t)"), start=True, stop=True)
                last.then_inc(stats_ps, 1)

            def keep_warm(n, ps):
                for _ in range(n):
                    nc.tensor.matmul(ps.rearrange("p (a q) -> p a q", q=P), ones_r[:, :],
                                     ones_r[:, :].unsqueeze(1).to_broadcast([P, 4, P]), start=True, stop=True)

            pe.wait_ge(ld_cst, 16)
            group_means(G0, HALF, bank[7], (C_GT, C_GT + P))
            pe.wait_ge(zeroed, 2)
            keep_warm(WARM_START, bank[0][:, :])

            def values():
                pe.wait_ge(w_pair_ready, 3)
                for ready in (g_low, g_copied):
                    pe.wait_ge(ready, len(RANGES))
                for x in range(W):
                    for src, w in ((g_pair, w_v_pair), (g_cross, w_v_cross)):
                        last = nc.tensor.matmul(bank[4 + x // 4][:, (x % 4) * P:(x % 4 + 1) * P].rearrange(
                            "p (a c) -> p a c", c=C), src[:, x + 1, 1:H + 1, :].rearrange("p y n -> p (y n)"),
                            w[:, :].unsqueeze(1).to_broadcast([P, 2, C]), start=(src is g_pair),
                            stop=(src is g_cross))
                last.then_inc(v_ps, 1)

            def conv_column(c, j):
                x = CHUNKS[c][0] + j
                if j == 0:
                    last_column = min(sum(CHUNKS[c]) + 2, PW - 1)
                    ranges = 1 + sum(xb <= last_column for _, xb in RANGES)
                    for ready in (g_low, g_copied):
                        pe.wait_ge(ready, ranges)
                if c and j == (2 if c == 1 else 0):
                    pe.wait_ge(u_ready, c)
                ps = bank[CONV_BANKS[c][j // 2]][:, (j % 2) * NCH:(j % 2 + 1) * NCH]
                for t in range(2 * KS):
                    ky, single = t // 2, t % 2
                    nc.tensor.matmul(ps, g_pair[:, x + 2 * single, ky:ky + H, :].rearrange("p y n -> p (y n)"),
                                     w_pair[:, t, :], start=(t == 0), stop=False)
                if c == 0 and j == 0:
                    pe.wait_ge(w_split, 2)
                for t in range(K2):
                    ky, kx = t // KS, t % KS
                    nc.tensor.matmul(ps, g_cross[:, x + kx, ky:ky + H, :].rearrange("p y n -> p (y n)"),
                                     w_cross[:, t, :], start=False, stop=False)
                last = nc.tensor.matmul(ps, ones_r[:, :], bias_r[:, :], start=False, stop=True)
                if j == CHUNKS[c][1] - 1:
                    last.then_inc(off_ps, 1)

            def tap_sum(c, g):
                q0, _, rows = GROUPS[g]
                n, size, _, out_ps = cell_blocks(c, g)
                cx = CHUNKS[c][1] * HEADS
                pe.wait_ge(prod_ready, (len(ROWS) - 1) * c + rows)
                for b in range(n):
                    for t in range(K2):
                        at = (t * CELLS + q0) * cx + b * size
                        last = nc.tensor.matmul(out_ps[0:size, b * P:(b + 1) * P], prod[:, at:at + size], ident,
                                                start=(b == 0 and t == 0), stop=(b == n - 1 and t == K2 - 1),
                                                is_transpose=True)
                last.then_inc(tap_ps, 1)

            def cells_back(c, g):
                q0, q1, _ = GROUPS[g]
                n, size, b0, _ = cell_blocks(c, g)
                cx = CHUNKS[c][1] * HEADS
                pe.wait_ge(cell_ts, len(GROUPS) * c + g + 1)
                out_ps = cells_ps(c, 0) if g == len(GROUPS) - 1 else cell_bank[:, q0 * cx:q1 * cx]
                for b in range(n):
                    last = nc.tensor.transpose(out_ps[:, b * size:(b + 1) * size], cell_t[0:size, b0 + b, :],
                                               cst[0:size, C_ID:C_ID + size])
                last.then_inc(cell_ps, 1)

            def row_sum(c, m):
                w, i = CHUNKS[c][1], APPLY[m]
                n = ND * c + m
                nd = 2 * DX[i] + 1
                pe.wait_ge(part_ready, n + 1)
                for d in range(nd):
                    for j in range(w // 2):
                        last = nc.tensor.matmul(comb_bank[:, j * P:(j + 1) * P], part[:, n % PARTS, d, j * P:(j + 1) * P], ident,
                                                start=(m == 0 and d == 0 and j == 0),
                                                stop=(m == ND - 1 and d == nd - 1 and j == w // 2 - 1),
                                                is_transpose=True)
                last.then_inc(part_used, 1)

            def project(out_banks, src, j0, j1, done):
                for par in range(2):
                    rows = slice(par * C, (par + 1) * C)
                    for half in range(2):
                        last = nc.tensor.matmul(
                            out_banks[par][half * C:(half + 1) * C, j0 * C:j1 * C], w_o_s[rows, :],
                            src[rows, j0:j1, :].rearrange("p j (y n) -> p j y n", n=N)[
                                :, :, :, half * HALF:(half + 1) * HALF], start=True, stop=True)
                last.then_inc(done, 1)

            def y0(c):
                x0, w = CHUNKS[c]
                pe.wait_ge(comb_ts, c + 1)
                project(y0_banks, comb_t, x0 // 2, (x0 + w) // 2, y0_ps)

            pe.wait_ge(w_high, 3)
            pe.wait_ge(w_pair_ready, 2)
            for c in range(2):
                for j in range(CHUNKS[c][1]):
                    conv_column(c, j)
                if c == 0:
                    values()
            pe.wait_ge(v_ready, 1)
            pe.wait_ge(ld_w0[3], 16)
            pending = [(c, j) for c in range(2, NC) for j in range(CHUNKS[c][1])]
            for c in range(NC):
                for k in range(BEFORE[c]):
                    conv_column(*pending.pop(0))
                if WARM_CHUNK[c]:
                    pe.wait_ge(u_ready, NC)
                    keep_warm(WARM_CHUNK[c], bank[0][:, :])
                tap_sum(c, 0)
                tap_sum(c, 1)
                cells_back(c, 0)
                tap_sum(c, 2)
                cells_back(c, 1)
                cells_back(c, 2)
                if c:
                    y0(c - 1)
                if c == NC - 1:
                    pe.wait_ge(flag_in, 1)
                    nc.tensor.matmul(bank[1][0:1, 0:2 * NC], ones[:, :],
                                     vflag[:, :, :].rearrange("p a c -> p (a c)"), start=True,
                                     stop=True).then_inc(flag_ps, 1)
                for m in range(ND):
                    if m < BETWEEN[c]:
                        conv_column(*pending.pop(0))
                    if c == NC - 1 and m == ND - 1:
                        pe.wait_ge(flag_sb, 1)
                        count = pe.value_load(vcount[0:1, 0:1], min_val=0, max_val=2 * NC * P)
                    row_sum(c, m)
            y0(NC - 1)
            with pe.If(count > 0):
                pe.wait_ge(far_ts, 1)
                for j in range(W // 2):
                    last = nc.tensor.transpose(bank[j // 4][:, (j % 4) * P:(j % 4 + 1) * P],
                                               far_sum[:, 2 * j:2 * j + 2, :].rearrange("p x c -> p (x c)"), ident)
                last.then_inc(far_tp, 1)
                pe.wait_ge(far_ts, 2)
                project(bank[2:4], far_t, 0, W // 2, far_y)

            keep_warm(WARM_IN[0], bank[0][:, :])
            group_means(G_IN, DUO, pair_stats(G_IN), (C_GB,))
            keep_warm(WARM_IN[1], bank[0][:, :])

            def images(ap, n=DUO):
                return ap.rearrange("p (n y x) -> p n y x", n=n, x=W)

            def conv(ps, n0, n, size, inputs, weights, low_ready, between=()):
                (in_h, in_l), (w_h, w_l) = inputs, weights
                for k, (src, w) in enumerate(((in_h, w_h), (in_h, w_l), (in_l, w_h))):
                    if k == 2:
                        pe.wait_ge(low_ready, n0 + n)
                    for t in range(size * size):
                        ky, kx = (t // size, t % size) if size == KS else (1, 1)
                        last = nc.tensor.matmul(images(ps, n), w(t), src[:, n0:n0 + n, ky:ky + H, kx:kx + W],
                                                start=(k == 0 and t == 0), stop=(k == 2 and t == size * size - 1))
                    if k < len(between):
                        between[k]()
                return last

            def second_mean():
                group_means(G_IN + 1, DUO, pair_stats(G_IN + 1), (C_GB,))

            def c1_mean():
                group_means(G_C1, DUO, pair_stats(G_C1), (C_GB,))

            def c1_mean_2():
                pe.wait_ge(caff_ready, 1)
                group_means(G_C1 + 2, DUO, pair_stats(G_C1 + 2), (C_GB,))

            def p_mean_2():
                group_means(G_P + 2, DUO, pair_stats(G_P + 2), (C_GB,))

            pe.wait_ge(low, 3)
            for g in range(2):
                n0 = DUO * g
                pe.wait_ge(g1_ready, n0 + DUO)
                conv(bank[g][:, :], n0, DUO, KS, (g1_h, g1_l), (lambda t: w12_h[:, t, :], lambda t: w12_l[:, t, :]),
                     g1_low, (second_mean if g == 0 else c1_mean,)).then_inc(r12_ps, 1)
                conv(bank[2 + g][:, :], n0, DUO, 1, (g1_h, g1_l), (lambda t: wc1_h[:, :], lambda t: wc1_l[:, :]),
                     g1_low).then_inc(c_ps, 1)
            pe.wait_ge(high, 7)
            pe.wait_ge(low, 4)
            for g in range(2):
                n0 = DUO * g
                pe.wait_ge(pooled_ready, g + 1)
                for t in range(2 * KS):
                    ky, kx = t // 2, 2 * (t % 2)
                    nc.tensor.matmul(images(bank[4 + g][:, :]), wp_pair[:, t, :],
                                     pool_pair[:, n0:n0 + DUO, ky:ky + H, kx:kx + W], start=(t == 0), stop=False)
                pe.wait_ge(pool_low, g + 1)
                pe.wait_ge(pool_copied, g + 1)
                for t in range(K2):
                    ky, kx = t // KS, t % KS
                    last = nc.tensor.matmul(images(bank[4 + g][:, :]), wp_cross[:, t, :],
                                            pool_cross[:, n0:n0 + DUO, ky:ky + H, kx:kx + W],
                                            start=False, stop=(t == K2 - 1))
                    if g == 1 and t == 5:
                        group_means(G_P, DUO, pair_stats(G_P), (C_GB,))
                last.then_inc(p_ps, 1)
            keep_warm(WARM_P, bank[0][:, :])
            for k, (i0, n) in enumerate(OUT_PARTS):
                pe.wait_ge(g2_ready, i0 + n)
                conv(out_banks[k][:, 0:n * HW], i0, n, KS, (g2_h, g2_l),
                     (lambda t: wc2_h[:, t, :], lambda t: wc2_l[:, t, :]), g2_low,
                     () if k else (c1_mean_2, p_mean_2)).then_inc(o_ps, 1)


_LAYOUT = ("x", "consts", "w_off", "w_v", "off_bias", "w_o", "w12", "b12", "wp", "wc1", "wc2", "vecs")


def kernel(**inputs):
    import numpy as _np
    import concourse.bacc as _bacc
    from concourse import mybir as _mybir
    from concourse.bass_utils import run_bass_kernel_spmd as _run

    a = {k: _np.asarray(v) for k, v in inputs.items()}
    l0 = {k[8:]: v for k, v in a.items() if k.startswith("L0_conv_")}
    l1 = {k[8:]: v for k, v in a.items() if k.startswith("L1_conv_")}

    def by_tap(off, attn):
        off = off.reshape((HEADS, K2, 2) + off.shape[1:])
        attn = attn.reshape((1, HEADS, K2) + attn.shape[1:])
        both = _np.concatenate([_np.moveaxis(off, 2, 0), attn])
        return _np.swapaxes(both, 1, 2).reshape((NCH,) + attn.shape[3:])

    w = by_tap(l0["off_w"], l0["attn_w"]).transpose(1, 2, 3, 0)
    w_off = w.reshape(C, K2, NCH)
    taps = lambda t: t.transpose(1, 2, 3, 0).reshape(t.shape[1], K2, t.shape[0])
    twice = lambda t: _np.concatenate([t, t])
    arrays = {
        "x": a["x"], "consts": shape_constants(), "w_off": w_off, "w_v": l0["Wv"].T,
        "off_bias": by_tap(l0["off_b"], l0["attn_b"]).reshape(1, NCH),
        "w_o": twice(l0["Wo"].T),
        "w12": _np.stack([taps(l1["p1_w"]), taps(l1["p2_w"])]),
        "b12": _np.concatenate([twice(l1["p1_b"]), twice(l1["p2_b"])]).reshape(P, 1),
        "wp": taps(l1["p_w"]), "wc1": l1["c1_w"][:, :, 0, 0].T, "wc2": taps(l1["c2_w"]),
        "vecs": _np.stack([twice(l1[k]) for k in ("p_gn_g", "p_gn_b", "gn1_g", "gn1_b", "c2_b")], 1),
    }
    nc = _bacc.Bacc("TRN2", target_bir_lowering=False, num_devices=1)
    feed, args = {}, []
    for name in _LAYOUT:
        t = _np.ascontiguousarray(arrays[name])
        feed[f"in_{name}"] = t
        args.append(nc.dram_tensor(f"in_{name}", t.shape, _mybir.dt.from_np(t.dtype), kind="ExternalInput").ap())
    args.append(nc.dram_tensor("out_0", (N, C, H, W), F32, kind="ExternalOutput").ap())
    build(nc, *args)
    return _run(nc, [feed], core_ids=[0]).results[0]["out_0"]
```
